# Optimizing a Trainium2 kernel written in Bass

```python
import numpy as np
import jax
import jax.numpy as jnp

def _softmax(x, axis=-1):
    return jax.nn.softmax(x, axis=axis)

def _gelu(x):
    return jax.nn.gelu(x, approximate=True)

def _silu(x):
    return jax.nn.silu(x)

def _sigmoid(x):
    return jax.nn.sigmoid(x)

def _layernorm(x, axis=-1, eps=1e-05):
    m = jnp.mean(x, axis=axis, keepdims=True)
    v = jnp.var(x, axis=axis, keepdims=True)
    return (x - m) / jnp.sqrt(v + eps)

def _scatter_add(tgt, idx, src, axis=0):
    return tgt.at[idx].add(src)

def _segment_sum(src, seg, n):
    return jax.ops.segment_sum(src, seg, n)
kernel_name = 'mk_seq_preln_d1_jaxref_r8_e2c8a8'

def setup_inputs(seed: int=0):
    np.random.seed(seed)
    _w = jnp.asarray

    def _L0_attn_setup():
        import jax, jax.numpy as jnp
        import numpy as np
        B, N, DIM = (4, 128, 128)
        H, DH, ORDER = (16, 64, 3)
        MAXREL = 64
        INNER = H * DH
        VOCAB = 2 * MAXREL + 1
        SCALE = DH ** (-0.5)
        TOPK = int(0.25 * N)
        key = jax.random.key(seed)
        ks = jax.random.split(key, 8)
        s = 0.02
        return {'x': jax.random.normal(ks[0], (B, N, DIM), jnp.float32), 'Wqkv': jax.random.normal(ks[1], (3 * INNER, DIM), jnp.float32) * s, 'bqkv': jnp.zeros((3 * INNER,), jnp.float32), 'Wout': jax.random.normal(ks[2], (DIM, INNER), jnp.float32) * s, 'bout': jnp.zeros((DIM,), jnp.float32), 'rel_k_emb': jax.random.normal(ks[3], (VOCAB, DH), jnp.float32) * s, 'rel_v_emb': jax.random.normal(ks[4], (VOCAB, DH), jnp.float32) * s, 'alphas_raw': jax.random.normal(ks[5], (ORDER, H), jnp.float32) * 0.5}
    _L0_attn_in = _L0_attn_setup()

    def _L0_ffn_setup():
        import jax, jax.numpy as jnp
        import numpy as np
        B, S, IN, OUT, E, R = (8, 512, 128, 128, 8, 8)
        LORA_ALPHA = 16
        SCALING = LORA_ALPHA / R
        key = jax.random.key(seed)
        k = jax.random.split(key, 6)
        x = jax.random.normal(k[0], (B, S, IN), dtype=jnp.float32)
        base_w = jax.random.normal(k[1], (OUT, IN), dtype=jnp.float32) * 0.02
        base_b = jnp.zeros((OUT,), dtype=jnp.float32)
        lora_A = jax.random.normal(k[2], (IN, R), dtype=jnp.float32) * 0.02
        lora_B = jax.random.normal(k[3], (E, R, OUT), dtype=jnp.float32) * 0.02
        router_w = jax.random.normal(k[4], (E, IN), dtype=jnp.float32) * 0.02
        router_b = jnp.zeros((E,), dtype=jnp.float32)
        return {'x': x, 'base_w': base_w, 'base_b': base_b, 'lora_A': lora_A, 'lora_B': lora_B, 'router_w': router_w, 'router_b': router_b}
    _L0_ffn_in = _L0_ffn_setup()
    _d = {'L0_attn_x': _L0_attn_in['x'], 'L0_attn_Wqkv': _L0_attn_in['Wqkv'], 'L0_attn_bqkv': _L0_attn_in['bqkv'], 'L0_attn_Wout': _L0_attn_in['Wout'], 'L0_attn_bout': _L0_attn_in['bout'], 'L0_attn_rel_k_emb': _L0_attn_in['rel_k_emb'], 'L0_attn_rel_v_emb': _L0_attn_in['rel_v_emb'], 'L0_attn_alphas_raw': _L0_attn_in['alphas_raw'], 'L0_ffn_base_w': _L0_ffn_in['base_w'], 'L0_ffn_base_b': _L0_ffn_in['base_b'], 'L0_ffn_lora_A': _L0_ffn_in['lora_A'], 'L0_ffn_lora_B': _L0_ffn_in['lora_B'], 'L0_ffn_router_w': _L0_ffn_in['router_w'], 'L0_ffn_router_b': _L0_ffn_in['router_b']}
    _x0 = _d['L0_attn_x']
    _d['L0_attn_x'] = jax.random.normal(jax.random.fold_in(jax.random.key(seed), 1), (8, 256, 128), dtype=_x0.dtype)
    del _x0
    return _d

def reference(L0_attn_x, L0_attn_Wqkv, L0_attn_bqkv, L0_attn_Wout, L0_attn_bout, L0_attn_rel_k_emb, L0_attn_rel_v_emb, L0_attn_alphas_raw, L0_ffn_base_w, L0_ffn_base_b, L0_ffn_lora_A, L0_ffn_lora_B, L0_ffn_router_w, L0_ffn_router_b):

    def _L0_attn_ref(x, Wqkv, bqkv, Wout, bout, rel_k_emb, rel_v_emb, alphas_raw):
        import jax, jax.numpy as jnp
        import numpy as np
        B, N, DIM = (4, 128, 128)
        H, DH, ORDER = (16, 64, 3)
        MAXREL = 64
        INNER = H * DH
        VOCAB = 2 * MAXREL + 1
        SCALE = DH ** (-0.5)
        TOPK = int(0.25 * N)
        b, n, _ = x.shape
        qkv = x @ Wqkv.T + bqkv
        q, k, v = jnp.split(qkv, 3, axis=-1)
        to_heads = lambda t: t.reshape(b, n, H, DH).transpose(0, 2, 1, 3)
        q, k, v = (to_heads(q), to_heads(k), to_heads(v))
        scores = jnp.einsum('bhid,bhjd->bhij', q, k) * SCALE
        coords = jnp.arange(n)
        dist = jnp.clip(coords[:, None] - coords[None, :], -MAXREL, MAXREL) + MAXREL
        rel_k = rel_k_emb[dist]
        scores = scores + jnp.einsum('bhid,ijd->bhij', q, rel_k)
        top_vals = jax.lax.top_k(scores, TOPK)[0]
        threshold = top_vals[..., -1:]
        scores = jnp.where(scores < threshold, -jnp.inf, scores)
        attn = jax.nn.softmax(scores, axis=-1)
        rel_v = rel_v_emb[dist]
        alphas = jax.nn.sigmoid(alphas_raw)
        res = jnp.zeros_like(v)
        v_curr = v
        for i in range(ORDER):
            a_v = jnp.einsum('bhij,bhjd->bhid', attn, v_curr)
            if i == 0:
                a_v = a_v + jnp.einsum('bhij,ijd->bhid', attn, rel_v)
            v_curr = a_v
            res = res + alphas[i][None, :, None, None] * v_curr
        out = res.transpose(0, 2, 1, 3).reshape(b, n, INNER)
        return out @ Wout.T + bout

    def _L0_ffn_ref(x, base_w, base_b, lora_A, lora_B, router_w, router_b):
        import jax, jax.numpy as jnp
        import numpy as np
        B, S, IN, OUT, E, R = (8, 512, 128, 128, 8, 8)
        LORA_ALPHA = 16
        SCALING = LORA_ALPHA / R
        result = jnp.einsum('bsd,od->bso', x, base_w) + base_b
        logits = jnp.einsum('bsd,ed->bse', x, router_w) + router_b
        gating = jax.nn.softmax(logits, axis=-1).astype(jnp.bfloat16)
        mid = jnp.einsum('bsd,dr->bsr', x, lora_A)
        lora_out = jnp.einsum('bsr,erd,bse->bsd', mid, lora_B, gating.astype(jnp.float32))
        return result + lora_out * SCALING
    x = L0_attn_x
    x = x + _L0_attn_ref(_layernorm(x, axis=-1), L0_attn_Wqkv, L0_attn_bqkv, L0_attn_Wout, L0_attn_bout, L0_attn_rel_k_emb, L0_attn_rel_v_emb, L0_attn_alphas_raw)
    x = x + _L0_ffn_ref(_layernorm(x, axis=-1), L0_ffn_base_w, L0_ffn_base_b, L0_ffn_lora_A, L0_ffn_lora_B, L0_ffn_router_w, L0_ffn_router_b)
    return x

_drawn_inputs = setup_inputs


def setup_inputs(seed=0):
    import zlib

    import numpy as np

    out = dict(_drawn_inputs(seed))
    spreads = {'L0_attn_bqkv': (0.0, 0.1),
     'L0_attn_bout': (0.0, 0.1),
     'L0_ffn_base_b': (0.0, 0.1),
     'L0_ffn_router_b': (0.0, 0.8)}
    factors = {'L0_attn_rel_k_emb': 5.604,
     'L0_attn_rel_v_emb': 6.806,
     'L0_attn_alphas_raw': 3.668,
     'L0_ffn_lora_A': 6.4,
     'L0_ffn_lora_B': 6.238,
     'L0_ffn_router_w': 8.0}
    for name, (base, spread) in spreads.items():
        noise = np.random.default_rng([zlib.crc32(name.encode()), seed]).standard_normal(out[name].shape)
        drawn = base * np.exp(spread * noise) if base else spread * noise
        out[name] = jnp.asarray(drawn.astype(out[name].dtype))
    for name, factor in factors.items():
        out[name] = (out[name] * factor).astype(out[name].dtype)
    return out
```

```python
import numpy as np
import concourse.bass as bass
from concourse import mybir
from contextlib import ExitStack


def preln_attention_ffn(nc: bass.Bass, x_d, wqkv_d, bv_d, wout_d, bout_d, relk_d, relv_d, alphas_d,
                        wffn_d, bffn_d, lorab_d, out_d):
    f32, bf16 = mybir.dt.float32, mybir.dt.bfloat16
    ALU, ACT = mybir.AluOpType, mybir.ActivationFunctionType
    AX = mybir.AxisListType

    B, N, DIM = x_d.shape
    P = 128
    DH = relv_d.shape[1]
    VOCAB = relv_d.shape[0]
    MAXREL = (VOCAB - 1) // 2
    NP = wqkv_d.shape[0]
    H = 2 * NP
    ORDER = alphas_d.shape[1] // H
    TOPK = 32
    ROUNDS = TOPK // 8
    SCALE = DH ** -0.5
    E_ = 8
    R_ = lorab_d.shape[0] // E_
    SCALING = 16 / R_
    EPS = 1e-5
    T = N // P
    TILES = B * T
    HEADS = B * H
    BODY = 4
    ITS = HEADS // BODY
    LOW = -3.0e38
    WIN = 192
    EXT = 2 * P + MAXREL - 1
    EDGE0, EDGE1 = MAXREL - 1, P - 1
    FFN = DIM + E_ + R_
    LATE = P + 2 * ORDER

    xT_d = nc.dram_tensor("xT_scratch", (P, B * N), f32).ap()
    cols_d = nc.dram_tensor("cols_scratch", (P, NP * 4), f32).ap()
    late_d = nc.dram_tensor("late_scratch", (NP, LATE), f32).ap()
    band_d = [nc.dram_tensor(f"band_scratch{i}", (P, T * EXT), f32).ap() for i in range(BODY)]
    diag_d = [nc.dram_tensor(f"diag_scratch{i}", (P, T * 2 * P), f32).ap() for i in range(BODY)]

    ctx = ExitStack()
    with ctx:
        def sb(name, shape, dt=f32):
            return ctx.enter_context(nc.sbuf_tensor(name, shape, dt))

        def sem(name):
            return ctx.enter_context(nc.semaphore(name))

        ident = sb("ident", [P, P])
        ones = sb("ones", [P, P])
        tri0 = sb("tri0", [DH, DH])
        tri1 = sb("tri1", [P, P])
        relk = sb("relk", [P, VOCAB])
        relk_end = sb("relk_end", [P, 2])
        relv = sb("relv", [P, DH])
        relv0 = sb("relv0", [P, DH])
        tailv = sb("tailv", [P, DH])
        colt = sb("colt", [P, NP, 4])
        bqk = sb("bqk", [P, NP, 2])
        late_sb = sb("late_sb", [1, NP, LATE])
        bv_sb = sb("bv_sb", [1, NP * P])
        al_sb = sb("al_sb", [1, NP * 2 * ORDER])
        zeros = sb("zeros", [P, 2 * P * T])
        x_sb = sb("x_sb", [P, TILES, DIM])
        stats = sb("stats", [P, TILES, 6])
        mv = sb("mv", [P, TILES, 2])
        std = sb("std", [P, TILES])
        rstd = sb("rstd", [P, TILES])
        xn = sb("xn", [P, TILES, DIM])
        xnT = sb("xnT", [P, B * N])
        w_sb = [sb(f"w_sb{i}", [P, 3 * P]) for i in range(2)]
        xT = [sb(f"xT{i}", [P, N]) for i in range(2)]
        cols = [sb(f"cols{i}", [P, 4]) for i in range(2)]
        late = [sb(f"late{i}", [P, LATE]) for i in range(2)]
        q_sb = [sb(f"q_sb{i}", [P, N]) for i in range(2)]
        k_sb = [sb(f"k_sb{i}", [P, N + 2 * MAXREL]) for i in range(2)]
        v_sb = [sb(f"v_sb{i}", [P, T, P]) for i in range(2)]
        band = [sb(f"band{i}", [P, T * EXT]) for i in range(BODY)]
        skew = [sb(f"skew{i}", [P, T, WIN]) for i in range(BODY)]
        top8 = [sb(f"top8_{i}", [P, T, ROUNDS * 8]) for i in range(2)]
        work = [sb(f"work{t}", [P, 2, N]) for t in range(T)]
        nmax = [sb(f"nmax{i}", [P, T]) for i in range(2)]
        rsum = [sb(f"rsum{i}", [P, T]) for i in range(2)]
        rinv = [sb(f"rinv{i}", [P, T]) for i in range(2)]
        e_sb = [sb(f"e_sb{i}", [P, T, N]) for i in range(2)]
        a_sb = [sb(f"a_sb{i}", [P, T, N]) for i in range(BODY)]
        aT = [sb(f"aT{i}", [P, T, N]) for i in range(2)]
        diag = [sb(f"diag{i}", [P, T, P]) for i in range(BODY)]
        diagT = [sb(f"diagT{i}", [P, N]) for i in range(2)]
        tail0 = [sb(f"tail0_{i}", [DH, P]) for i in range(2)]
        tail1 = [sb(f"tail1_{i}", [P, P]) for i in range(2)]
        tailx = sb("tailx", [DH, DH])
        v1 = [sb(f"v1_{i}", [P, T, DH]) for i in range(2)]
        v2 = [sb(f"v2_{i}", [P, T, DH]) for i in range(2)]
        u1 = [sb(f"u1_{i}", [P, T, DH]) for i in range(2)]
        u2 = [sb(f"u2_{i}", [P, T, DH]) for i in range(2)]
        u3 = [sb(f"u3_{i}", [P, T, DH]) for i in range(2)]
        u12 = sb("u12", [P, T, DH])
        res = sb("res", [P, HEADS, T, DH])
        wout = sb("wout", [P, NP, DIM])
        bout = sb("bout", [P, DIM])
        wffn = sb("wffn", [P, FFN])
        bffn = sb("bffn", [P, DIM + E_])
        lorab = sb("lorab", [E_ * R_, DIM])
        rcur = [sb(f"rcur{t}", [P, H, DH]) for t in range(T)]
        rT = [sb(f"rT{t}", [P, NP, P]) for t in range(T)]
        y_sb = x_sb
        agg = [sb(f"agg{t}", [P, 2]) for t in range(T)]
        yn = [sb(f"yn{t}", [P, DIM]) for t in range(T)]
        ynT = [sb(f"ynT{t}", [P, P]) for t in range(T)]
        base = [sb(f"base{t}", [P, FFN]) for t in range(T)]
        lmax = [sb(f"lmax{t}", [P, 1]) for t in range(T)]
        gate = [sb(f"gate{t}", [P, E_]) for t in range(T)]
        gsum = [sb(f"gsum{t}", [P, 2]) for t in range(T)]
        gbf = [sb(f"gbf{t}", [P, E_], bf16) for t in range(T)]
        z_sb = [sb(f"z_sb{t}", [P, P]) for t in range(T)]
        zT = [sb(f"zT{t}", [E_ * R_, P]) for t in range(T)]
        o_sb = [sb(f"o_sb{t}", [P, DIM]) for t in range(T)]

        def pb(name):
            return ctx.enter_context(nc.psum_tensor(name, [P, 512], f32))

        ps_s = [pb("ps_s0"), pb("ps_s1")]
        ps_t = [pb("ps_t0"), pb("ps_t1")]
        ps_qk, ps_p, ps_gv, ps_r = pb("ps_qk"), pb("ps_p"), pb("ps_gv"), pb("ps_r")
        ps_g, ps_v = ps_gv[:, 0:N], ps_gv[:, N:2 * N]

        ps_y, ps_f = [ps_r, ps_qk], [ps_p, ps_gv]

        consts_in = sem("consts_in")
        x_in = sem("x_in")
        made = sem("made")
        scratch_zero = sem("scratch_zero")
        tables = sem("tables")
        alpha_exp = sem("alpha_exp")
        tables_out = sem("tables_out")
        dve_p = sem("dve_p")
        std_done = sem("std_done")
        xn_done = sem("xn_done")
        xnT_ready = sem("xnT_ready")
        xnT_saved = sem("xnT_saved")
        xT_out = sem("xT_out")
        pair_in = [sem("pair_in0"), sem("pair_in1")]
        late_in = [sem("late_in0"), sem("late_in1")]
        qk_ready, qk_saved = sem("qk_ready"), sem("qk_saved")
        v_ready, v_saved, v_biased = sem("v_ready"), sem("v_saved"), sem("v_biased")
        p_ready, band_saved, edges = sem("p_ready"), sem("band_saved"), sem("edges")
        band_out = [sem(f"band_out{i}") for i in range(BODY)]
        skew_in = [sem(f"skew_in{i}") for i in range(BODY)]
        s_ready = sem("s_ready")
        top_step = sem("top_step")
        nmax_done, exp_done = sem("nmax_done"), sem("exp_done")
        masked, rinv_done = sem("masked"), sem("rinv_done")
        normed = sem("normed")
        diag_out = [sem(f"diag_out{i}") for i in range(BODY)]
        diag_in = [sem(f"diag_in{i}") for i in range(BODY)]
        t_ready, t_saved = sem("t_ready"), sem("t_saved")
        g_ready, g_saved = sem("g_ready"), sem("g_saved")
        tails = sem("tails")
        r1_ready, r2_ready, r3_ready = sem("r1_ready"), sem("r2_ready"), sem("r3_ready")
        r1_saved, r2_saved, r3_saved = sem("r1_saved"), sem("r2_saved"), sem("r3_saved")
        u_done = sem("u_done")
        summed = sem("summed")
        passed = sem("passed")
        xb_done = sem("xb_done")
        rcur_done = sem("rcur_done")
        rT_ready, rT_saved = sem("rT_ready"), sem("rT_saved")
        y_ready, y_done = sem("y_ready"), sem("y_done")
        y_stats = sem("y_stats")
        std2_done = sem("std2_done")
        yn_done, ynT_ready, ynT_saved = sem("yn_done"), sem("ynT_ready"), sem("ynT_saved")
        f_ready, f_saved = sem("f_ready"), sem("f_saved")
        lmax_done, gate_exp = sem("lmax_done"), sem("gate_exp")
        z_done, zT_ready, zT_saved = sem("z_done"), sem("zT_ready"), sem("zT_saved")
        l_ready, o_done = sem("l_ready"), sem("o_done")
        out_sent = [sem(f"out_sent{t}") for t in range(T)]

        block = ctx.enter_context(nc.Block())

        def sweep(eng, slot):
            for it in (-1, 0, 1):
                for s in range(BODY):
                    slot(it, s)
            with eng.Fori(2, ITS - 2) as it:
                for s in range(BODY):
                    slot(it, s)
            for it in (ITS - 2, ITS - 1, ITS):
                for s in range(BODY):
                    slot(it, s)

        def there(it, s):
            return not isinstance(it, int) or 0 <= BODY * it + s < HEADS

        def wait(eng, semaphore, each, it, s):
            if not isinstance(it, int) or BODY * it + s >= 0:
                eng.wait_ge(semaphore, it * (BODY * each) + (s + 1) * each)

        def wait_pair(eng, semaphore, each, it, s):
            if not isinstance(it, int) or BODY * it + s >= 0:
                eng.wait_ge(semaphore, it * (2 * each) + (s // 2 + 1) * each)

        def wait_dma(eng, ring, it, s):
            if not isinstance(it, int) or BODY * it + s >= 0:
                eng.wait_ge(ring[s % BODY], it * 16 + (s // BODY + 1) * 16)

        def wait_pair_dma(eng, ring, each, it, s):
            if not isinstance(it, int) or BODY * it + s >= 0:
                p = s // 2
                eng.wait_ge(ring[p % 2], it * each + (p // 2 + 1) * each)

        def batches(eng, body):
            body(0)
            with eng.Fori(1, B) as b:
                body(b)

        def reach(eng, semaphore, value):
            if not isinstance(value, int) or value > 0:
                eng.wait_ge(semaphore, value)

        def settle(eng):
            eng.sem_inc(passed)

        CONSTS = 13

        @block.sync
        def _(sp):
            sp.dma_start(x_sb[:], x_d.rearrange("b (t p) d -> p (b t) d", p=P)).then_inc(x_in, 16)
            for dst, src in ((relk[0:DH, :], relk_d), (relk[DH:P, :], relk_d), (relv[:], relv_d[0:P, :]),
                             (relv0[:], relv_d[P:P + 1, :].to_broadcast([P, DH])),
                             (tailv[:], relv_d[0:1, :].to_broadcast([P, DH])),
                             (bqk[:], wqkv_d[:, :, 3 * P:3 * P + 2].rearrange("h p c -> p h c")),
                             (bv_sb[:], bv_d), (al_sb[:], alphas_d),
                             (wout[:], wout_d.rearrange("(h p) n -> p h n", p=P)),
                             (bout[:], bout_d.to_broadcast([P, DIM])), (wffn[:], wffn_d),
                             (bffn[:], bffn_d.to_broadcast([P, DIM + E_])), (lorab[:], lorab_d)):
                sp.dma_start(dst, src).then_inc(consts_in, 16)
            sp.wait_ge(made, 6)
            for i in range(BODY):
                sp.dma_start(diag_d[i], zeros[:]).then_inc(scratch_zero, 16)
            sp.wait_ge(tables, 1)
            sp.dma_start(cols_d, colt[:].rearrange("p h c -> p (h c)")).then_inc(tables_out, 16)
            sp.dma_start(late_d.rearrange("h c -> (h c)").unsqueeze(0), late_sb[:].rearrange("p h c -> p (h c)")).then_inc(tables_out, 16)
            sp.wait_ge(xnT_saved, TILES // 4)
            sp.dma_start(xT_d, xnT[:]).then_inc(xT_out, 16)
            sp.wait_ge(xT_out, 16)
            sp.wait_ge(tables_out, 32)
            sp.wait_ge(scratch_zero, 16 * BODY)

            def load_pair(it, s):
                par = (s // 2) % 2
                pair = it * 2 + s // 2
                hp, b = pair % NP, pair // NP
                wait_pair(sp, v_ready, 1, it, s - 4)
                settle(sp)
                wait_pair(sp, qk_saved, 4, it, s - 4)
                settle(sp)
                sp.dma_start(w_sb[par][:], wqkv_d[bass.ds(hp, 1), :, 0:3 * P].rearrange("h p c -> p (h c)")
                             ).then_inc(pair_in[par], 16)
                sp.dma_start(cols[par][:], cols_d[:, bass.ds(hp * 4, 4)]).then_inc(pair_in[par], 16)
                sp.dma_start(xT[par][:], xT_d[:, bass.ds(b * N, N)]).then_inc(pair_in[par], 16)

            def load_late(it, s):
                par = (s // 2) % 2
                hp = (it * 2 + s // 2) % NP
                wait_pair(sp, v_biased, 1, it, s - 4)
                settle(sp)
                wait(sp, u_done, 2, it, s - 3)
                settle(sp)
                sp.dma_start(late[par][:], late_d[bass.ds(hp, 1), :].to_broadcast([P, LATE])
                             ).then_inc(late_in[par], 16)

            load_pair(0, 0)

            def slot(it, s):
                if there(it, s - 1):
                    r = (s - 1) % BODY
                    wait(sp, normed, T, it, s - 1)
                    settle(sp)
                    wait_dma(sp, diag_in, it, s - 1 - BODY)
                    src = a_sb[r][:].rearrange("p t n -> p (t n)")
                    src = bass.AP(src.tensor, 0, [[T * N, P], [N + MAXREL, T], [1, WIN]])
                    dst = bass.AP(diag_d[r].tensor, MAXREL, [[T * 2 * P, P], [WIN, T], [1, WIN]])
                    sp.dma_start(dst, src).then_inc(diag_out[r], 16)
                if there(it, s + 2):
                    r = (s + 2) % BODY
                    wait_dma(sp, band_out, it, s + 2)
                    settle(sp)
                    wait(sp, s_ready, 1, it, s + 2 - BODY)
                    src = bass.AP(band_d[r].tensor, P - 1, [[T * EXT - 1, P], [EXT, T], [1, WIN]])
                    sp.dma_start(skew[r][:], src).then_inc(skew_in[r], 16)
                if there(it, s - 1):
                    r = (s - 1) % BODY
                    wait_dma(sp, diag_out, it, s - 1)
                    settle(sp)
                    wait(sp, g_ready, 1, it, s - 1 - BODY)
                    src = bass.AP(diag_d[r].tensor, 0, [[T * 2 * P + 1, P], [2 * P, T], [1, P]])
                    sp.dma_start(diag[r][:], src).then_inc(diag_in[r], 16)
                if s % 2 == 0 and there(it, s):
                    load_late(it, s)
                if there(it, s + 3):
                    r = (s + 3) % BODY
                    wait(sp, edges, 4, it, s + 3)
                    settle(sp)
                    wait_dma(sp, skew_in, it, s + 3 - BODY)
                    sp.dma_start(band_d[r], band[r][:]).then_inc(band_out[r], 16)
                if s % 2 == 0 and there(it, s + 6):
                    load_pair(it, s + 6)

            sweep(sp, slot)

            def send(b):
                for t in range(T):
                    reach(sp, o_done, b * T + (t + 1))
                    settle(sp)
                    sp.dma_start(out_d[bass.ds(b, 1), t * P:(t + 1) * P, :].rearrange("b p d -> p (b d)"),
                                 o_sb[t][:]).then_inc(out_sent[t], 16)

            batches(sp, send)
            for t in range(T):
                sp.wait_ge(out_sent[t], 16 * B)

        @block.gpsimd
        def _(pool):
            nc.gpsimd.memset(ones[:], 1.0).then_inc(made, 1)
            pool.wait_ge(made, 1)
            nc.gpsimd.affine_select(out=ident[:], in_=ones[:], compare_op=ALU.is_equal, fill=0.0, base=0,
                                    pattern=[[-1, P]], channel_multiplier=1).then_inc(made, 1)
            nc.gpsimd.affine_select(out=tri0[:], in_=ones[0:DH, 0:DH], compare_op=ALU.is_ge, fill=0.0, base=-1,
                                    pattern=[[1, DH]], channel_multiplier=-1).then_inc(made, 1)
            nc.gpsimd.affine_select(out=tri1[:], in_=ones[:], compare_op=ALU.is_ge, fill=0.0, base=MAXREL - 1,
                                    pattern=[[1, P]], channel_multiplier=-1).then_inc(made, 1)
            for i in range(2):
                last = nc.gpsimd.memset(tail0[i][:], 0.0)
            last.then_inc(made, 1)
            nc.gpsimd.memset(zeros[:], 0.0).then_inc(made, 1)
            pool.wait_ge(x_in, 16)
            pool.wait_ge(consts_in, 16 * CONSTS)
            pool.wait_ge(made, 6)

            def slot(it, s):
                if there(it, s - 1):
                    r, par = (s - 1) % BODY, (s - 1) % 2
                    wait(pool, rinv_done, 1, it, s - 1)
                    settle(pool)
                    for t in range(T):
                        nc.gpsimd.tensor_scalar(a_sb[r][:, t, :], a_sb[r][:, t, :], rinv[par][:, t:t + 1], 1.0,
                                                ALU.mult, ALU.mult).then_inc(normed, 1)
                if there(it, s - 2):
                    par = s % 2
                    wait(pool, t_saved, 1, it, s - 2)
                    wait(pool, r1_ready, 1, it, s - 4)
                    wait(pool, tails, 4, it, s - 3)
                    nc.gpsimd.tensor_tensor(tail0[par][:, DH:P], aT[par][0:DH, 0, DH:P], tri0[:],
                                            ALU.mult).then_inc(tails, 1)
                    nc.gpsimd.tensor_tensor(tail1[par][:], aT[par][:, 0, P:2 * P], tri1[:],
                                            ALU.mult).then_inc(tails, 1)
                    nc.gpsimd.tensor_tensor(tailx[:], aT[par][0:DH, 1, P + DH:2 * P], tri0[:],
                                            ALU.mult).then_inc(tails, 1)
                    pool.wait_ge(tails, it * (4 * BODY) + (4 * (s - 2) + 3))
                    nc.gpsimd.tensor_tensor(tail1[par][0:DH, DH:P], tail1[par][0:DH, DH:P], tailx[:],
                                            ALU.add).then_inc(tails, 1)
                if there(it, s - 3):
                    par = (s - 3) % 2
                    wait(pool, u_done, 2, it, s - 3)
                    wait(pool, summed, 2, it, s - 4)
                    nc.gpsimd.tensor_tensor(u12[:], u1[par][:], u2[par][:], ALU.add).then_inc(summed, 1)
                    pool.wait_ge(summed, it * (2 * BODY) + (2 * (s - 3) + 1))
                    settle(pool)
                    nc.gpsimd.tensor_tensor(res[:, bass.ds(it * BODY + (s - 3), 1), :, :].rearrange("p k t d -> p (k t d)"),
                                            u12[:].rearrange("p t d -> p (t d)"),
                                            u3[par][:].rearrange("p t d -> p (t d)"), ALU.add).then_inc(summed, 1)
                if s % 2 == 1 and there(it, s - 1):
                    par = ((s - 1) // 2) % 2
                    wait_pair(pool, v_saved, 1, it, s - 1)
                    wait_pair_dma(pool, late_in, 16, it, s - 1)
                    nc.gpsimd.tensor_tensor(v_sb[par][:], v_sb[par][:],
                                            late[par][:, 0:P].unsqueeze(1).to_broadcast([P, T, P]),
                                            ALU.add).then_inc(v_biased, 1)
                if there(it, s + 3):
                    r = (s + 3) % BODY
                    wait(pool, band_saved, 1, it, s + 3)
                    settle(pool)
                    for t, left in ((0, EDGE0), (1, EDGE1)):
                        o, right = t * EXT, EXT - VOCAB - left
                        for a, n, c in ((o, left, o + left), (o + left + VOCAB, right, o + left + VOCAB - 1)):
                            nc.gpsimd.tensor_scalar(band[r][:, a:a + n], ones[:, 0:n], band[r][:, c:c + 1], 1.0,
                                                    ALU.mult, ALU.mult).then_inc(edges, 1)

            sweep(pool, slot)

            pool.wait_ge(xn_done, TILES)
            nc.gpsimd.tensor_tensor(x_sb[:], x_sb[:], bout[:].unsqueeze(1).to_broadcast([P, TILES, DIM]),
                                    ALU.add).then_inc(xb_done, 1)
            pool.wait_ge(summed, 2 * HEADS)

            def gather(b):
                for t in range(T):
                    reach(pool, rT_ready, (b - 1) * (2 * T) + (2 * t + 2))
                    nc.gpsimd.tensor_copy(rcur[t][:], res[:, bass.ds(b * H, H), t, :]).then_inc(rcur_done, 1)

            batches(pool, gather)

        @block.scalar
        def _(act):
            act.wait_ge(consts_in, 16 * CONSTS)
            nc.scalar.activation(late_sb[:, :, P:LATE], al_sb[:].rearrange("p (h c) -> p h c", h=NP), ACT.Exp,
                                 scale=-1.0).then_inc(alpha_exp, 1)
            act.wait_ge(dve_p, 2 * TILES + 1)
            nc.scalar.activation(std[:], mv[:, :, 1], ACT.Sqrt).then_inc(std_done, 1)
            for g in range(TILES // 4):
                act.wait_ge(xnT_ready, g + 1)
                nc.scalar.copy(xnT[:, g * 4 * P:(g + 1) * 4 * P], ps_s[g % 2][:]).then_inc(xnT_saved, 1)

            def slot(it, s):
                if there(it, s - 2):
                    par = s % 2
                    wait(act, g_ready, 1, it, s - 2)
                    wait(act, r1_ready, 1, it, s - 4)
                    nc.scalar.copy(diagT[par][:], ps_g).then_inc(g_saved, 1)
                if there(it, s):
                    par = s % 2
                    wait(act, nmax_done, 1, it, s)
                    wait(act, masked, T, it, s - 2)
                    for t in range(T):
                        nc.scalar.activation(e_sb[par][:, t, :], ps_s[par][:, t * N:(t + 1) * N], ACT.Exp,
                                             bias=nmax[par][:, t:t + 1], scale=1.0).then_inc(exp_done, 1)
                if there(it, s - 1):
                    par = (s - 1) % 2
                    wait(act, t_ready, 1, it, s - 1)
                    wait(act, r3_ready, 1, it, s - 3)
                    wait(act, tails, 4, it, s - 3)
                    nc.scalar.copy(aT[par][:].rearrange("p c n -> p (c n)"), ps_t[par][:]).then_inc(t_saved, 1)
                if there(it, s + 3):
                    r = (s + 3) % BODY
                    wait(act, p_ready, 1, it, s + 3)
                    wait_dma(act, band_out, it, s + 3 - BODY)
                    dst = bass.AP(band[r][:].tensor, EDGE0, [[T * EXT, P], [EXT + EDGE1 - EDGE0, T], [1, VOCAB]])
                    nc.scalar.copy(dst, ps_p[:, 0:T * VOCAB].rearrange("p (t c) -> p t c", t=T)).then_inc(band_saved, 1)

                def alpha(j):
                    c = P + (s % 2) * ORDER + j
                    return late[((s - 2) // 2) % 2][:, c:c + 1]

                flat = "p t d -> p (t d)"
                if there(it, s - 2):
                    par = s % 2
                    wait(act, r1_ready, 1, it, s - 2)
                    wait(act, summed, 2, it, s - 4)
                    if s % 2 == 0:
                        wait_pair_dma(act, late_in, 16, it, s - 2)
                    nc.scalar.copy(v1[par][:].rearrange(flat), ps_r[:, 0:P]).then_inc(r1_saved, 1)
                if s % 2 == 0 and there(it, s + 4):
                    par = (s // 2) % 2
                    wait_pair(act, qk_ready, 1, it, s + 4)
                    wait(act, s_ready, 1, it, s + 1)
                    c = cols[par]
                    nc.scalar.activation(q_sb[par][:], ps_qk[:, 0:N], ACT.Identity, bias=c[:, 0:1],
                                         scale=1.0).then_inc(qk_saved, 1)
                    for a, n, src, col in ((0, MAXREL, 0, 2), (MAXREL, N, 0, 1), (MAXREL + N, MAXREL, N - MAXREL, 3)):
                        nc.scalar.activation(k_sb[par][:, a:a + n], ps_qk[:, N + src:N + src + n], ACT.Identity,
                                             bias=c[:, col:col + 1], scale=SCALE).then_inc(qk_saved, 1)
                if there(it, s - 2):
                    par = s % 2
                    wait(act, r2_ready, 1, it, s - 2)
                    nc.scalar.copy(v2[par][:].rearrange(flat), ps_r[:, P:2 * P]).then_inc(r2_saved, 1)
                    wait(act, r1_saved, 1, it, s - 2)
                    nc.scalar.activation(u1[par][:].rearrange(flat), v1[par][:].rearrange(flat), ACT.Copy,
                                         scale=alpha(0)).then_inc(u_done, 1)
                if s % 2 == 1 and there(it, s + 1):
                    par = ((s + 1) // 2) % 2
                    wait_pair(act, v_ready, 1, it, s + 1)
                    wait(act, r1_ready, 1, it, s - 2)
                    nc.scalar.copy(v_sb[par][:].rearrange("p t d -> p (t d)"), ps_v).then_inc(v_saved, 1)
                if there(it, s - 2):
                    par = s % 2
                    wait(act, r3_ready, 1, it, s - 2)
                    nc.scalar.activation(u3[par][:].rearrange(flat), ps_r[:, 2 * P:3 * P], ACT.Copy,
                                         scale=alpha(2)).then_inc(r3_saved, 1)
                    wait(act, r2_saved, 1, it, s - 2)
                    nc.scalar.activation(u2[par][:].rearrange(flat), v2[par][:].rearrange(flat), ACT.Copy,
                                         scale=alpha(1)).then_inc(u_done, 1)

            sweep(act, slot)

            def save_res(b):
                for t in range(T):
                    for half in range(2):
                        reach(act, y_ready, (b - 1) * T + (t + 1))
                        act.wait_ge(rT_ready, b * (2 * T) + (2 * t + half + 1))
                        nc.scalar.copy(rT[t][:, half * NP // 2:(half + 1) * NP // 2, :].rearrange("p h n -> p (h n)"),
                                       ps_s[half][:]).then_inc(rT_saved, 1)

            batches(act, save_res)
            act.wait_ge(y_stats, 1)
            nc.scalar.activation(std[:], mv[:, :, 1], ACT.Sqrt).then_inc(std2_done, 1)

            def second(b):
                for t in range(T):
                    act.wait_ge(ynT_ready, b * T + (t + 1))
                    nc.scalar.copy(ynT[t][:], ps_t[t][:, 0:P]).then_inc(ynT_saved, 1)
                    act.wait_ge(lmax_done, b * T + (t + 1))
                    nc.scalar.activation(gate[t][:], base[t][:, DIM:DIM + E_], ACT.Exp, bias=lmax[t][:, 0:1],
                                         scale=1.0, accum_out=gsum[t][:, 0:1]).then_inc(gate_exp, 1)
                    act.wait_ge(zT_ready, b * T + (t + 1))
                    nc.scalar.mul(zT[t][:], ps_t[t][0:E_ * R_, P:2 * P], SCALING).then_inc(zT_saved, 1)

            batches(act, second)

        @block.vector
        def _(dve):
            steps = [0]

            def own(ins):
                steps[0] += 1
                ins.then_inc(dve_p, 1)
                dve.wait_ge(dve_p, steps[0])

            dve.wait_ge(x_in, 16)
            for i in range(TILES):
                own(nc.vector.bn_stats(stats[:, i, :], x_sb[:, i, :]))
                own(nc.vector.bn_aggr(mv[:, i, :], stats[:, i, :]))
            own(nc.vector.tensor_scalar(mv[:, :, 1], mv[:, :, 1], EPS, None, ALU.add))
            dve.wait_ge(consts_in, 16 * CONSTS)
            own(nc.vector.tensor_tensor(relv[:], relv[:], relv0[:], ALU.subtract))
            own(nc.vector.tensor_tensor(tailv[:], tailv[:], relv0[:], ALU.subtract))
            own(nc.vector.tensor_copy(colt[:, :, 0], bqk[:, :, 0]))
            own(nc.vector.tensor_scalar(colt[:, :, 1], bqk[:, :, 1], SCALE, None, ALU.mult))
            own(nc.vector.tensor_scalar(colt[:, :, 2], colt[:, :, 1], relk[:, 0:1], None, ALU.add))
            own(nc.vector.tensor_scalar(colt[:, :, 3], colt[:, :, 1], relk[:, VOCAB - 1:VOCAB], None, ALU.add))
            own(nc.vector.tensor_tensor(late_sb[:, :, 0:DH], bv_sb[:].rearrange("p (h c) -> p h c", h=NP)[:, :, 0:DH],
                                        relv0[0:1, :].unsqueeze(1).to_broadcast([1, NP, DH]), ALU.add))
            own(nc.vector.tensor_tensor(late_sb[:, :, DH:P], bv_sb[:].rearrange("p (h c) -> p h c", h=NP)[:, :, DH:P],
                                        relv0[0:1, :].unsqueeze(1).to_broadcast([1, NP, DH]), ALU.add))
            dve.wait_ge(alpha_exp, 1)
            own(nc.vector.tensor_scalar(late_sb[:, :, P:LATE], late_sb[:, :, P:LATE], 1.0, None, ALU.add))
            own(nc.vector.reciprocal(late_sb[:, :, P:LATE], late_sb[:, :, P:LATE]))
            for t in range(T):
                last = nc.vector.memset(z_sb[t][:], 0.0)
            last.then_inc(tables, 1)
            dve.wait_ge(std_done, 1)
            own(nc.vector.reciprocal(rstd[:], std[:]))
            for i in range(TILES):
                nc.vector.tensor_scalar(xn[:, i, :], x_sb[:, i, :], mv[:, i, 0:1], rstd[:, i:i + 1],
                                        ALU.subtract, ALU.mult).then_inc(xn_done, 1)

            STEPS = T * (2 * ROUNDS - 1)

            def slot(it, s):
                if not there(it, s):
                    return
                par, r = s % 2, s % BODY
                m = top8[par]

                def own_step(i):
                    dve.wait_ge(top_step, i + 1)

                wait(dve, s_ready, 1, it, s)
                settle(dve)
                if there(it, s - 1):
                    dve.wait_ge(top_step, STEPS)
                    dve.sem_clear(top_step)
                step = 0
                for n in range(ROUNDS):
                    for t in range(T):
                        src = ps_s[par][:, t * N:(t + 1) * N] if n == 0 else work[t][:, (n - 1) % 2, :]
                        if n:
                            own_step(step - T)
                        nc.vector.max(m[:, t, 8 * n:8 * n + 8], src).then_inc(top_step, 1)
                        step += 1
                    if n < ROUNDS - 1:
                        for t in range(T):
                            src = ps_s[par][:, t * N:(t + 1) * N] if n == 0 else work[t][:, (n - 1) % 2, :]
                            own_step(step - T)
                            nc.vector.match_replace(work[t][:, n % 2, :], m[:, t, 8 * n:8 * n + 8], src,
                                                    LOW).then_inc(top_step, 1)
                            step += 1
                    if n == 0:
                        wait(dve, exp_done, T, it, s - 2)
                        nc.vector.tensor_scalar(nmax[par][:], m[:, :, 0], -1.0, None, ALU.mult).then_inc(nmax_done, 1)
                wait(dve, exp_done, T, it, s)
                wait(dve, t_ready, 1, it, s - BODY)
                wait_dma(dve, diag_out, it, s - BODY)
                wait(dve, normed, T, it, s - 2)
                for t in range(T):
                    own_step(step - T + t)
                    nc.vector.scalar_tensor_tensor(a_sb[r][:, t, :], ps_s[par][:, t * N:(t + 1) * N],
                                                   m[:, t, TOPK - 1:TOPK], e_sb[par][:, t, :], ALU.is_ge, ALU.mult,
                                                   accum_out=rsum[par][:, t:t + 1]).then_inc(masked, 1)
                wait(dve, masked, T, it, s)
                nc.vector.reciprocal(rinv[par][:], rsum[par][:]).then_inc(rinv_done, 1)

            sweep(dve, slot)

            dve.wait_ge(xb_done, 1)
            base_steps = steps[0]
            def add_attention(b):
                for t in range(T):
                    i = b * T + t
                    dve.wait_ge(y_ready, b * T + (t + 1))
                    y = y_sb[:, bass.ds(i, 1), :].rearrange("p i d -> p (i d)")
                    nc.vector.tensor_tensor(y, ps_y[t][:, 0:P], y, ALU.add).then_inc(y_done, 1)
                    dve.wait_ge(y_done, b * T + (t + 1))
                    settle(dve)
                    nc.vector.bn_stats(stats[:, t, :], y).then_inc(dve_p, 1)
                    dve.wait_ge(dve_p, b * (3 * T) + (base_steps + 3 * t + 1))
                    settle(dve)
                    nc.vector.bn_aggr(agg[t][:], stats[:, t, :]).then_inc(dve_p, 1)
                    dve.wait_ge(dve_p, b * (3 * T) + (base_steps + 3 * t + 2))
                    settle(dve)
                    nc.vector.tensor_copy(mv[:, bass.ds(i, 1), :].rearrange("p i d -> p (i d)"), agg[t][:]).then_inc(dve_p, 1)
                    dve.wait_ge(dve_p, b * (3 * T) + (base_steps + 3 * t + 3))

            batches(dve, add_attention)
            nc.vector.tensor_scalar(mv[:, :, 1], mv[:, :, 1], EPS, None, ALU.add).then_inc(y_stats, 1)
            dve.wait_ge(std2_done, 1)
            base2 = base_steps + 3 * TILES
            nc.vector.reciprocal(rstd[:], std[:]).then_inc(dve_p, 1)
            dve.wait_ge(dve_p, base2 + 1)

            def second(b):
                for t in range(T):
                    i = b * T + t
                    k0 = base2 + 1 + 3 * t
                    y = y_sb[:, bass.ds(i, 1), :].rearrange("p i d -> p (i d)")
                    nc.vector.tensor_scalar(yn[t][:], y, mv[:, bass.ds(i, 1), 0:1].rearrange("p i d -> p (i d)"),
                                            rstd[:, bass.ds(i, 1)], ALU.subtract, ALU.mult).then_inc(yn_done, 1)
                    dve.wait_ge(f_ready, b * T + (t + 1))
                    nc.vector.tensor_tensor(base[t][:, 0:DIM + E_], ps_f[t][:, 0:DIM + E_], bffn[:],
                                            ALU.add).then_inc(dve_p, 1)
                    nc.vector.tensor_copy(base[t][:, DIM + E_:FFN], ps_f[t][:, DIM + E_:FFN]).then_inc(dve_p, 1)
                    dve.wait_ge(dve_p, b * (3 * T) + (k0 + 2))
                    nc.vector.tensor_reduce(lmax[t][:], base[t][:, DIM:DIM + E_], AX.X, ALU.max, negate=True).then_inc(lmax_done, 1)
                    dve.wait_ge(gate_exp, b * T + (t + 1))
                    nc.vector.reciprocal(gsum[t][:, 1:2], gsum[t][:, 0:1]).then_inc(dve_p, 1)
                    dve.wait_ge(dve_p, b * (3 * T) + (k0 + 3))
                    nc.vector.tensor_scalar(gbf[t][:], gate[t][:], gsum[t][:, 1:2], None, ALU.mult).then_inc(f_saved, 1)
                    dve.wait_ge(f_saved, b * T + (t + 1))
                    nc.vector.tensor_tensor(z_sb[t][:, 0:E_ * R_].rearrange("p (e r) -> p e r", e=E_), gbf[t][:].unsqueeze(2).to_broadcast([P, E_, R_]),
                                            base[t][:, DIM + E_:FFN].unsqueeze(1).to_broadcast([P, E_, R_]),
                                            ALU.mult).then_inc(z_done, 1)
                    dve.wait_ge(l_ready, b * T + (t + 1))
                    nc.vector.tensor_tensor(base[t][:, 0:DIM], base[t][:, 0:DIM], y, ALU.add).then_inc(y_done, 1)
                    dve.wait_ge(y_done, b * T + (TILES + t + 1))
                    reach(dve, out_sent[t], b * 16)
                    nc.vector.tensor_tensor(o_sb[t][:], ps_y[t][:, 0:P], base[t][:, 0:DIM],
                                            ALU.add).then_inc(o_done, 1)

            batches(dve, second)

        @block.tensor
        def _(pe):
            mm, transpose = nc.tensor.matmul, nc.tensor.transpose
            pe.wait_ge(made, 6)
            for g in range(TILES // 4):
                pe.wait_ge(xn_done, 4 * (g + 1))
                if g >= 2:
                    pe.wait_ge(xnT_saved, g - 1)
                for i in range(4):
                    last = transpose(ps_s[g % 2][:, i * P:(i + 1) * P], xn[:, 4 * g + i, :], ident[:])
                last.then_inc(xnT_ready, 1)
            pe.wait_ge(xnT_saved, TILES // 4)
            pe.wait_ge(tables, 1)

            def slot(it, s):
                if there(it, s + 1):
                    j = s + 1
                    par, r, pair, h = j % 2, j % BODY, (j // 2) % 2, (j % 2) * DH
                    wait_dma(pe, skew_in, it, j)
                    wait(pe, masked, T, it, j - 2)
                    q, k, d = q_sb[pair], k_sb[pair], skew[r]
                    far = (MAXREL + N, 0)
                    near = (MAXREL, 2 * MAXREL)
                    for t in range(T):
                        lhsT = q[h:h + DH, t * P:(t + 1) * P]
                        o = t * N
                        a, f = (o, o + WIN) if t == 0 else (o + N - WIN, o)
                        mm(ps_s[par][:, a:a + WIN], lhsT, k[h:h + DH, near[t]:near[t] + WIN], start=True, stop=False)
                        mm(ps_s[par][:, a:a + WIN], ident[:], d[:, t, :], start=False, stop=True)
                        last = mm(ps_s[par][:, f:f + N - WIN], lhsT, k[h:h + DH, far[t]:far[t] + N - WIN],
                                  start=True, stop=True)
                    last.then_inc(s_ready, 1)
                if there(it, s - 2):
                    r = (s - 2) % BODY
                    wait_dma(pe, diag_in, it, s - 2)
                    wait(pe, g_saved, 1, it, s - 3)
                    if s % 2 == 0 and there(it, s):
                        wait_pair(pe, v_saved, 1, it, s)
                    for t in range(T):
                        last = transpose(ps_g[:, t * P:(t + 1) * P], diag[r][:, t, :], ident[:])
                    last.then_inc(g_ready, 1)
                if there(it, s - 1):
                    r, par = (s - 1) % BODY, (s - 1) % 2
                    wait(pe, normed, T, it, s - 1)
                    wait(pe, t_saved, 1, it, s - 3)
                    for c in range(T):
                        for t in range(T):
                            last = transpose(ps_t[par][:, c * N + t * P:c * N + (t + 1) * P],
                                             a_sb[r][:, t, c * P:(c + 1) * P], ident[:])
                    last.then_inc(t_ready, 1)
                if there(it, s + 3):
                    j = s + 3
                    pair, h = (j // 2) % 2, (j % 2) * DH
                    wait_pair(pe, qk_saved, 4, it, j)
                    wait(pe, band_saved, 1, it, j - 1)
                    for t in range(T):
                        last = mm(ps_p[:, t * VOCAB:(t + 1) * VOCAB], q_sb[pair][h:h + DH, t * P:(t + 1) * P],
                                  relk[h:h + DH, :], start=True, stop=True)
                    last.then_inc(p_ready, 1)

                def power(src, col, ready):
                    for t in range(T):
                        for c in range(T):
                            last = mm(ps_r[:, col + t * DH:col + (t + 1) * DH], aT[par][:, c, t * P:(t + 1) * P],
                                      src[:, c, :], start=(c == 0), stop=(c == T - 1))
                    last.then_inc(ready, 1)

                par = s % 2
                if there(it, s - 2):
                    j = s - 2
                    pair, h = (j // 2) % 2, (j % 2) * DH
                    wait(pe, t_saved, 1, it, j)
                    wait(pe, g_saved, 1, it, j)
                    wait(pe, tails, 4, it, j)
                    wait_pair(pe, v_biased, 1, it, j)
                    wait(pe, r3_saved, 1, it, j - 1)
                    for t in range(T):
                        out = ps_r[:, t * DH:(t + 1) * DH]
                        for c in range(T):
                            mm(out, aT[par][:, c, t * P:(t + 1) * P], v_sb[pair][:, c, h:h + DH],
                               start=(c == 0), stop=False)
                        mm(out, diagT[par][:, t * P:(t + 1) * P], relv[:], start=False, stop=False)
                        if t == 0:
                            last = mm(out, tail0[par][:], tailv[0:DH, :], start=False, stop=True)
                        else:
                            last = mm(out, tail1[par][:], tailv[:], start=False, stop=True)
                    last.then_inc(r1_ready, 1)
                if s % 2 == 0 and there(it, s + 4):
                    pair = (s // 2) % 2
                    wait_pair_dma(pe, pair_in, 48, it, s + 4)
                    wait_pair(pe, qk_saved, 4, it, s + 2)
                    mm(ps_qk[:, 0:N], w_sb[pair][:, 0:P], xT[pair][:], start=True, stop=True)
                    mm(ps_qk[:, N:2 * N], w_sb[pair][:, P:2 * P], xT[pair][:], start=True,
                       stop=True).then_inc(qk_ready, 1)
                if there(it, s - 2):
                    wait(pe, r1_saved, 1, it, s - 2)
                    power(v1[par], P, r2_ready)
                if s % 2 == 0 and there(it, s + 2):
                    pair = ((s + 2) // 2) % 2
                    wait_pair(pe, v_saved, 1, it, s)
                    wait(pe, g_saved, 1, it, s - 2)
                    for c in range(T):
                        last = mm(ps_v[:, c * P:(c + 1) * P], xT[pair][:, c * P:(c + 1) * P],
                                  w_sb[pair][:, 2 * P:3 * P], start=True, stop=True)
                    last.then_inc(v_ready, 1)
                if there(it, s - 2):
                    wait(pe, r2_saved, 1, it, s - 2)
                    power(v2[par], 2 * P, r3_ready)

            sweep(pe, slot)

            pe.wait_ge(r3_saved, HEADS)
            pe.wait_ge(masked, T * HEADS)
            def project(b):
                for t in range(T):
                    pe.wait_ge(rcur_done, b * T + (t + 1))
                    for half in range(2):
                        reach(pe, rT_saved, b * (2 * T) + (2 * t + half - 1))
                        for i in range(NP // 2):
                            h = half * NP // 2 + i
                            last = transpose(ps_s[half][:, i * P:(i + 1) * P],
                                             rcur[t][:, 2 * h:2 * h + 2, :].rearrange("p a d -> p (a d)"), ident[:])
                        last.then_inc(rT_ready, 1)
                    pe.wait_ge(rT_saved, b * (2 * T) + (2 * t + 2))
                    reach(pe, y_done, (b - 1) * T + (t + 1))
                    for h in range(NP):
                        last = mm(ps_y[t][:, 0:P], rT[t][:, h, :], wout[:, h, :],
                                  start=(h == 0), stop=(h == NP - 1))
                    last.then_inc(y_ready, 1)

            batches(pe, project)
            pe.wait_ge(y_done, TILES)

            def second(b):
                for t in range(T):
                    pe.wait_ge(yn_done, b * T + (t + 1))
                    transpose(ps_t[t][:, 0:P], yn[t][:], ident[:]).then_inc(ynT_ready, 1)
                    pe.wait_ge(ynT_saved, b * T + (t + 1))
                    mm(ps_f[t][:, 0:FFN], ynT[t][:], wffn[:], start=True, stop=True).then_inc(f_ready, 1)
                    pe.wait_ge(z_done, b * T + (t + 1))
                    transpose(ps_t[t][:, P:2 * P], z_sb[t][:], ident[:]).then_inc(zT_ready, 1)
                    pe.wait_ge(zT_saved, b * T + (t + 1))
                    mm(ps_y[t][:, 0:P], zT[t][:], lorab[:], start=True, stop=True).then_inc(l_ready, 1)

            batches(pe, second)


def kernel(L0_attn_x, L0_attn_Wqkv, L0_attn_bqkv, L0_attn_Wout, L0_attn_bout, L0_attn_rel_k_emb,
           L0_attn_rel_v_emb, L0_attn_alphas_raw, L0_ffn_base_w, L0_ffn_base_b, L0_ffn_lora_A, L0_ffn_lora_B,
           L0_ffn_router_w, L0_ffn_router_b):
    import concourse.bacc as bacc
    from concourse.bass_utils import run_bass_kernel_spmd

    f = {k: np.asarray(v) for k, v in dict(
        x=L0_attn_x, wqkv=L0_attn_Wqkv, bqkv=L0_attn_bqkv, wout=L0_attn_Wout, bout=L0_attn_bout,
        relk=L0_attn_rel_k_emb, relv=L0_attn_rel_v_emb, alphas=L0_attn_alphas_raw, bw=L0_ffn_base_w,
        bb=L0_ffn_base_b, la=L0_ffn_lora_A, lb=L0_ffn_lora_B, rw=L0_ffn_router_w, rb=L0_ffn_router_b).items()}
    inner, dim = f["wqkv"].shape[0] // 3, f["wqkv"].shape[1]
    pairs = inner // 128
    w = f["wqkv"].reshape(3, pairs, 128, dim).transpose(1, 3, 0, 2).reshape(pairs, dim, 3 * 128)
    bqk = f["bqkv"].reshape(3, pairs, 128)[:2].transpose(1, 2, 0)
    ins = {
        "x": f["x"],
        "wqkv": np.concatenate([w, bqk], axis=2),
        "bv": f["bqkv"][None, 2 * inner:],
        "wout": f["wout"].T,
        "bout": f["bout"][None, :],
        "relk": f["relk"][::-1].T,
        "relv": f["relv"][::-1],
        "alphas": f["alphas"].T.reshape(1, -1),
        "wffn": np.concatenate([f["bw"].T, f["rw"].T, f["la"]], axis=1),
        "bffn": np.concatenate([f["bb"], f["rb"]])[None, :],
        "lorab": f["lb"].reshape(-1, f["lb"].shape[2]),
    }
    nc = bacc.Bacc("TRN2", target_bir_lowering=False, num_devices=1)
    arrays, args = {}, []
    for name, a in ins.items():
        a = np.ascontiguousarray(a)
        arrays[f"in_{name}"] = a
        args.append(nc.dram_tensor(f"in_{name}", a.shape, mybir.dt.from_np(a.dtype), kind="ExternalInput").ap())
    args.append(nc.dram_tensor("out_0", f["x"].shape, mybir.dt.float32, kind="ExternalOutput").ap())
    preln_attention_ffn(nc, *args)
    r = run_bass_kernel_spmd(nc, [arrays], core_ids=[0])
    return r.results[0]["out_0"]
```

```python
import numpy as np
import concourse.bass as bass
from concourse import mybir
from contextlib import ExitStack


def preln_attention_ffn(nc: bass.Bass, x_d, wqkv_d, bv_d, wout_d, bout_d, relk_d, relv_d, alphas_d,
                        wffn_d, bffn_d, lorab_d, out_d):
    f32, bf16 = mybir.dt.float32, mybir.dt.bfloat16
    ALU, ACT = mybir.AluOpType, mybir.ActivationFunctionType
    AX = mybir.AxisListType

    B, N, DIM = x_d.shape
    P = 128
    DH = relv_d.shape[1]
    VOCAB = relv_d.shape[0]
    MAXREL = (VOCAB - 1) // 2
    NP = wqkv_d.shape[0]
    H = 2 * NP
    ORDER = alphas_d.shape[1] // H
    TOPK = 32
    ROUNDS = TOPK // 8
    SCALE = DH ** -0.5
    E_ = 8
    R_ = lorab_d.shape[0] // E_
    SCALING = 16 / R_
    EPS = 1e-5
    T = N // P
    TILES = B * T
    HEADS = B * H
    BODY = 4
    ITS = HEADS // BODY
    LOW = -3.0e38
    WIN = 192
    EXT = 2 * P + MAXREL - 1
    EDGE0, EDGE1 = MAXREL - 1, P - 1
    FFN = DIM + E_ + R_
    LATE = P + 2 * ORDER

    xT_d = nc.dram_tensor("xT_scratch", (P, B * N), f32).ap()
    cols_d = nc.dram_tensor("cols_scratch", (P, NP * 4), f32).ap()
    late_d = nc.dram_tensor("late_scratch", (NP, LATE), f32).ap()
    band_d = [nc.dram_tensor(f"band_scratch{i}", (P, T * EXT), f32).ap() for i in range(BODY)]
    diag_d = [nc.dram_tensor(f"diag_scratch{i}", (P, T * 2 * P), f32).ap() for i in range(BODY)]

    ctx = ExitStack()
    with ctx:
        def sb(name, shape, dt=f32):
            return ctx.enter_context(nc.sbuf_tensor(name, shape, dt))

        def sem(name):
            return ctx.enter_context(nc.semaphore(name))

        ident = sb("ident", [P, P])
        ones = sb("ones", [P, WIN])
        left = sb("left", [P, MAXREL + WIN])
        relk = sb("relk", [P, VOCAB])
        relv = sb("relv", [P, 2, DH])
        relv0 = sb("relv0", [P, DH])
        colt = sb("colt", [P, NP, 4])
        bqk = sb("bqk", [P, NP, 2])
        late_sb = sb("late_sb", [1, NP, LATE])
        bv_sb = sb("bv_sb", [1, NP * P])
        al_sb = sb("al_sb", [1, NP * 2 * ORDER])
        zeros = sb("zeros", [P, 2 * P * T])
        x_sb = sb("x_sb", [P, TILES, DIM])
        stats = sb("stats", [P, TILES, 6])
        mv = sb("mv", [P, TILES, 2])
        std = sb("std", [P, TILES])
        rstd = sb("rstd", [P, TILES])
        xn = sb("xn", [P, TILES, DIM])
        xnT = sb("xnT", [P, B * N])
        w_sb = [sb(f"w_sb{i}", [P, 3 * P]) for i in range(2)]
        xT = [sb(f"xT{i}", [P, N]) for i in range(2)]
        cols = [sb(f"cols{i}", [P, 4]) for i in range(2)]
        late = [sb(f"late{i}", [P, LATE]) for i in range(2)]
        q_sb = [sb(f"q_sb{i}", [P, N]) for i in range(2)]
        k_sb = [sb(f"k_sb{i}", [P, T, N]) for i in range(2)]
        v_sb = [sb(f"v_sb{i}", [P, T, P]) for i in range(2)]
        band = [sb(f"band{i}", [P, T * EXT]) for i in range(BODY)]
        skew = [sb(f"skew{i}", [P, T, N]) for i in range(BODY)]
        s_sb = [sb(f"s_sb{i}", [P, T, N]) for i in range(BODY)]
        top8 = [sb(f"top8_{i}", [P, T, ROUNDS * 8]) for i in range(2)]
        work = [sb(f"work{t}", [P, 2, N]) for t in range(T)]
        nmax = [sb(f"nmax{i}", [P, T]) for i in range(2)]
        rsum = [sb(f"rsum{i}", [P, T]) for i in range(2)]
        rinv = [sb(f"rinv{i}", [P, T]) for i in range(2)]
        e_sb = [sb(f"e_sb{i}", [P, T, N]) for i in range(2)]
        a_sb = [sb(f"a_sb{i}", [P, T, N]) for i in range(BODY)]
        aT = [sb(f"aT{i}", [P, T, N]) for i in range(2)]
        lefts = [sb(f"lefts{i}", [P, MAXREL + WIN]) for i in range(2)]
        diag = [sb(f"diag{i}", [P, T, P + 1]) for i in range(BODY)]
        diagT = [sb(f"diagT{i}", [P, N]) for i in range(2)]
        v1 = sb("v1", [P, T, 2, DH])
        v2 = sb("v2", [P, T, 2, DH])
        u1 = sb("u1", [P, T, DH])
        u2 = [sb(f"u2_{i}", [P, T, DH]) for i in range(2)]
        u3 = [sb(f"u3_{i}", [P, T, DH]) for i in range(2)]
        u23 = sb("u23", [P, T, DH])
        res = sb("res", [P, HEADS, T, DH])
        wout = sb("wout", [P, NP, DIM])
        bout = sb("bout", [P, DIM])
        wffn = sb("wffn", [P, FFN])
        bffn = sb("bffn", [P, DIM + E_])
        lorab = sb("lorab", [E_ * R_, DIM])
        rcur = [sb(f"rcur{t}", [P, H, DH]) for t in range(T)]
        rT = [sb(f"rT{t}", [P, NP, P]) for t in range(T)]
        y_sb = x_sb
        agg = [sb(f"agg{t}", [P, 2]) for t in range(T)]
        yn = [sb(f"yn{t}", [P, DIM]) for t in range(T)]
        ynT = [sb(f"ynT{t}", [P, P]) for t in range(T)]
        base = [sb(f"base{t}", [P, FFN]) for t in range(T)]
        lmax = [sb(f"lmax{t}", [P, 1]) for t in range(T)]
        gate = [sb(f"gate{t}", [P, E_]) for t in range(T)]
        gsum = [sb(f"gsum{t}", [P, 2]) for t in range(T)]
        gbf = [sb(f"gbf{t}", [P, E_], bf16) for t in range(T)]
        z_sb = [sb(f"z_sb{t}", [P, P]) for t in range(T)]
        zT = [sb(f"zT{t}", [E_ * R_, P]) for t in range(T)]
        o_sb = [sb(f"o_sb{t}", [P, DIM]) for t in range(T)]

        def pb(name):
            return ctx.enter_context(nc.psum_tensor(name, [P, 512], f32))

        ps_s, ps_t, ps_g, ps_qk, ps_p, ps_v = (pb(n) for n in ("ps_s", "ps_t", "ps_g", "ps_qk", "ps_p", "ps_v"))
        ps_r = ctx.enter_context(nc.psum_tensor("ps_r", [P, T, 512], f32))

        ps_x, ps_e, ps_f = [ps_s, ps_qk], [ps_t, ps_g], [ps_p, ps_v]
        ps_y = [ps_r[:, t, 0:DIM] for t in range(T)]

        consts_in = sem("consts_in")
        x_in = sem("x_in")
        made = sem("made")
        scratch_zero = sem("scratch_zero")
        tables = sem("tables")
        alpha_exp = sem("alpha_exp")
        tables_out = sem("tables_out")
        dve_p = sem("dve_p")
        std_done = sem("std_done")
        xn_done = sem("xn_done")
        xnT_ready = sem("xnT_ready")
        xnT_saved = sem("xnT_saved")
        xT_out = sem("xT_out")
        pair_in = [sem("pair_in0"), sem("pair_in1")]
        late_in = [sem("late_in0"), sem("late_in1")]
        qk_ready, qk_saved = sem("qk_ready"), sem("qk_saved")
        v_ready, v_saved, v_biased = sem("v_ready"), sem("v_saved"), sem("v_biased")
        p_ready, band_saved = sem("p_ready"), sem("band_saved")
        band_out = [sem(f"band_out{i}") for i in range(BODY)]
        skew_in = [sem(f"skew_in{i}") for i in range(BODY)]
        s_ready, s_saved = sem("s_ready"), sem("s_saved")
        s_added = sem("s_added")
        top_step = sem("top_step")
        nmax_done, exp_done = sem("nmax_done"), sem("exp_done")
        masked, rinv_done = sem("masked"), sem("rinv_done")
        normed = sem("normed")
        diag_out = [sem(f"diag_out{i}") for i in range(BODY)]
        diag_in = [sem(f"diag_in{i}") for i in range(BODY)]
        t_ready, t_saved = sem("t_ready"), sem("t_saved")
        g_ready, g_saved = sem("g_ready"), sem("g_saved")
        left_done, left_summed = sem("left_done"), sem("left_summed")
        r1_ready, r2_ready, r3_ready = sem("r1_ready"), sem("r2_ready"), sem("r3_ready")
        r1_saved, r2_saved, r3_saved = sem("r1_saved"), sem("r2_saved"), sem("r3_saved")
        u_done = sem("u_done")
        summed = sem("summed")
        passed = sem("passed")
        xb_done = sem("xb_done")
        rcur_done = sem("rcur_done")
        rT_ready, rT_saved = sem("rT_ready"), sem("rT_saved")
        y_ready, y_done = sem("y_ready"), sem("y_done")
        y_stats = sem("y_stats")
        std2_done = sem("std2_done")
        yn_done, ynT_ready, ynT_saved = sem("yn_done"), sem("ynT_ready"), sem("ynT_saved")
        f_ready, f_saved = sem("f_ready"), sem("f_saved")
        lmax_done, gate_exp = sem("lmax_done"), sem("gate_exp")
        z_done, zT_ready, zT_saved = sem("z_done"), sem("zT_ready"), sem("zT_saved")
        l_ready, o_done = sem("l_ready"), sem("o_done")
        out_sent = [sem(f"out_sent{t}") for t in range(T)]

        block = ctx.enter_context(nc.Block())

        def sweep(eng, slot):
            for it in (-1, 0, 1):
                for s in range(BODY):
                    slot(it, s)
            with eng.Fori(2, ITS - 2) as it:
                for s in range(BODY):
                    slot(it, s)
            for it in (ITS - 2, ITS - 1, ITS):
                for s in range(BODY):
                    slot(it, s)

        def there(it, s):
            return not isinstance(it, int) or 0 <= BODY * it + s < HEADS

        def wait(eng, semaphore, each, it, s):
            if not isinstance(it, int) or BODY * it + s >= 0:
                eng.wait_ge(semaphore, it * (BODY * each) + (s + 1) * each)

        def wait_pair(eng, semaphore, each, it, s):
            if not isinstance(it, int) or BODY * it + s >= 0:
                eng.wait_ge(semaphore, it * (2 * each) + (s // 2 + 1) * each)

        def wait_dma(eng, ring, it, s):
            if not isinstance(it, int) or BODY * it + s >= 0:
                eng.wait_ge(ring[s % BODY], it * 16 + (s // BODY + 1) * 16)

        def wait_pair_dma(eng, ring, each, it, s):
            if not isinstance(it, int) or BODY * it + s >= 0:
                p = s // 2
                eng.wait_ge(ring[p % 2], it * each + (p // 2 + 1) * each)

        def batches(eng, body):
            body(0)
            with eng.Fori(1, B) as b:
                body(b)

        def reach(eng, semaphore, value):
            if not isinstance(value, int) or value > 0:
                eng.wait_ge(semaphore, value)

        def settle(eng):
            eng.sem_inc(passed)

        CONSTS = 13
        MADE = 7 + BODY

        @block.sync
        def _(sp):
            sp.dma_start(x_sb[:], x_d.rearrange("b (t p) d -> p (b t) d", p=P)).then_inc(x_in, 16)
            for dst, src in ((relk[0:DH, :], relk_d), (relk[DH:P, :], relk_d), (relv[:, 0, :], relv_d[0:P, :]), (relv[:, 1, :], relv_d[0:P, :]),
                             (relv0[:], relv_d[P:P + 1, :].to_broadcast([P, DH])),
                             (bqk[:], wqkv_d[:, :, 3 * P:3 * P + 2].rearrange("h p c -> p h c")),
                             (bv_sb[:], bv_d), (al_sb[:], alphas_d),
                             (wout[:], wout_d.rearrange("(h p) n -> p h n", p=P)),
                             (bout[:], bout_d.to_broadcast([P, DIM])), (wffn[:], wffn_d),
                             (bffn[:], bffn_d.to_broadcast([P, DIM + E_])), (lorab[:], lorab_d)):
                sp.dma_start(dst, src).then_inc(consts_in, 16)
            sp.wait_ge(made, MADE)
            for i in range(BODY):
                sp.dma_start(diag_d[i], zeros[:]).then_inc(scratch_zero, 16)
            sp.wait_ge(tables, 1)
            sp.dma_start(cols_d, colt[:].rearrange("p h c -> p (h c)")).then_inc(tables_out, 16)
            sp.dma_start(late_d.rearrange("h c -> (h c)").unsqueeze(0), late_sb[:].rearrange("p h c -> p (h c)")).then_inc(tables_out, 16)
            sp.wait_ge(xnT_saved, TILES // 4)
            sp.dma_start(xT_d, xnT[:]).then_inc(xT_out, 16)
            sp.wait_ge(xT_out, 16)
            sp.wait_ge(tables_out, 32)
            sp.wait_ge(scratch_zero, 16 * BODY)

            def load_pair(it, s):
                par = (s // 2) % 2
                pair = it * 2 + s // 2
                hp, b = pair % NP, pair // NP
                wait_pair(sp, v_ready, 1, it, s - 4)
                settle(sp)
                wait_pair(sp, qk_saved, 5, it, s - 4)
                settle(sp)
                sp.dma_start(w_sb[par][:], wqkv_d[bass.ds(hp, 1), :, 0:3 * P].rearrange("h p c -> p (h c)")
                             ).then_inc(pair_in[par], 16)
                sp.dma_start(cols[par][:], cols_d[:, bass.ds(hp * 4, 4)]).then_inc(pair_in[par], 16)
                sp.dma_start(xT[par][:], xT_d[:, bass.ds(b * N, N)]).then_inc(pair_in[par], 16)

            def load_late(it, s):
                par = (s // 2) % 2
                hp = (it * 2 + s // 2) % NP
                wait_pair(sp, v_biased, 1, it, s - 4)
                settle(sp)
                wait(sp, u_done, 1, it, s - 3)
                settle(sp)
                wait(sp, r3_saved, 1, it, s - 3)
                settle(sp)
                wait(sp, summed, 3, it, s - 3)
                settle(sp)
                sp.dma_start(late[par][:], late_d[bass.ds(hp, 1), :].to_broadcast([P, LATE])
                             ).then_inc(late_in[par], 16)

            load_pair(0, 0)

            def slot(it, s):
                if there(it, s - 1):
                    r = (s - 1) % BODY
                    wait(sp, normed, T, it, s - 1)
                    settle(sp)
                    wait_dma(sp, diag_in, it, s - 1 - BODY)
                    src = a_sb[r][:].rearrange("p t n -> p (t n)")
                    src = bass.AP(src.tensor, 0, [[T * N, P], [N + MAXREL, T], [1, WIN]])
                    dst = bass.AP(diag_d[r].tensor, MAXREL, [[T * 2 * P, P], [WIN, T], [1, WIN]])
                    sp.dma_start(dst, src).then_inc(diag_out[r], 16)
                if there(it, s + 2):
                    r = (s + 2) % BODY
                    wait_dma(sp, band_out, it, s + 2)
                    settle(sp)
                    wait(sp, s_added, 1, it, s + 2 - BODY)
                    src = bass.AP(band_d[r].tensor, P - 1, [[T * EXT - 1, P], [EXT, T], [1, WIN]])
                    dst = bass.AP(skew[r][:].tensor, 0, [[T * N, P], [N + MAXREL, T], [1, WIN]])
                    sp.dma_start(dst, src).then_inc(skew_in[r], 16)
                if s % 2 == 0 and there(it, s):
                    load_late(it, s)
                if s % 2 == 1 and there(it, s + 5):
                    load_pair(it, s + 5)
                if there(it, s - 1):
                    r = (s - 1) % BODY
                    wait_dma(sp, diag_out, it, s - 1)
                    settle(sp)
                    wait(sp, g_ready, 1, it, s - 1 - BODY)
                    src = bass.AP(diag_d[r].tensor, 1, [[T * 2 * P + 1, P], [2 * P, T], [1, P]])
                    sp.dma_start(diag[r][:, :, 1:P + 1], src).then_inc(diag_in[r], 16)
                if there(it, s + 3):
                    r = (s + 3) % BODY
                    wait(sp, band_saved, 5, it, s + 3)
                    settle(sp)
                    wait_dma(sp, skew_in, it, s + 3 - BODY)
                    sp.dma_start(band_d[r], band[r][:]).then_inc(band_out[r], 16)

            sweep(sp, slot)

            def send(b):
                for t in range(T):
                    reach(sp, o_done, b * T + (t + 1))
                    settle(sp)
                    sp.dma_start(out_d[bass.ds(b, 1), t * P:(t + 1) * P, :].rearrange("b p d -> p (b d)"),
                                 o_sb[t][:]).then_inc(out_sent[t], 16)

            batches(sp, send)
            for t in range(T):
                sp.wait_ge(out_sent[t], 16 * B)

        @block.gpsimd
        def _(pool):
            nc.gpsimd.memset(ones[:], 1.0).then_inc(made, 1)
            pool.wait_ge(made, 1)
            nc.gpsimd.affine_select(out=ident[:], in_=ones[:, 0:P], compare_op=ALU.is_equal, fill=0.0, base=0,
                                    pattern=[[-1, P]], channel_multiplier=1).then_inc(made, 1)
            for a, n, base in ((0, MAXREL, -MAXREL), (MAXREL, WIN, P - MAXREL)):
                nc.gpsimd.affine_select(out=left[:, a:a + n], in_=ones[:, 0:n], compare_op=ALU.is_ge, fill=0.0,
                                        base=base, pattern=[[-1, n]], channel_multiplier=1).then_inc(made, 1)
            nc.gpsimd.memset(v1[:], 0.0).then_inc(made, 1)
            nc.gpsimd.memset(v2[:], 0.0).then_inc(made, 1)
            for i in range(BODY):
                nc.gpsimd.memset(skew[i][:], 0.0).then_inc(made, 1)
            nc.gpsimd.memset(zeros[:], 0.0).then_inc(made, 1)
            pool.wait_ge(x_in, 16)
            pool.wait_ge(consts_in, 16 * CONSTS)
            pool.wait_ge(made, MADE)

            def slot(it, s):
                if there(it, s - 1):
                    r, par = (s - 1) % BODY, (s - 1) % 2
                    wait(pool, rinv_done, 1, it, s - 1)
                    settle(pool)
                    for t in range(T):
                        nc.gpsimd.tensor_scalar(a_sb[r][:, t, :], a_sb[r][:, t, :], rinv[par][:, t:t + 1], 1.0,
                                                ALU.mult, ALU.mult).then_inc(normed, 1)
                if there(it, s - 1):
                    r, par = (s - 1) % BODY, (s - 1) % 2
                    wait(pool, left_summed, T, it, s - 3)
                    wait(pool, normed, T, it, s - 1)
                    nc.gpsimd.tensor_tensor(lefts[par][:, 0:MAXREL], a_sb[r][:, 0, 0:MAXREL], left[:, 0:MAXREL],
                                            ALU.mult).then_inc(left_done, 1)
                    nc.gpsimd.tensor_tensor(lefts[par][:, MAXREL:MAXREL + WIN], a_sb[r][:, 1, 0:WIN],
                                            left[:, MAXREL:MAXREL + WIN], ALU.mult).then_inc(left_done, 1)
                if there(it, s + 1):
                    r = (s + 1) % BODY
                    wait_dma(pool, skew_in, it, s + 1)
                    wait(pool, s_saved, 1, it, s + 1)
                    nc.gpsimd.tensor_tensor(s_sb[r][:], s_sb[r][:], skew[r][:], ALU.add).then_inc(s_added, 1)
                if s % 2 == 1 and there(it, s - 1):
                    par = ((s - 1) // 2) % 2
                    wait_pair(pool, v_saved, 1, it, s - 1)
                    wait_pair_dma(pool, late_in, 16, it, s - 1)
                    nc.gpsimd.tensor_tensor(v_sb[par][:], v_sb[par][:],
                                            late[par][:, 0:P].unsqueeze(1).to_broadcast([P, T, P]),
                                            ALU.add).then_inc(v_biased, 1)
                if there(it, s - 3):
                    par = (s - 3) % 2
                    c = P + ((s - 3) % 2) * ORDER
                    alpha0 = late[((s - 3) // 2) % 2][:, c:c + 1]
                    wait_pair_dma(pool, late_in, 16, it, s - 3)
                    wait(pool, u_done, 1, it, s - 3)
                    settle(pool)
                    wait(pool, r3_saved, 1, it, s - 3)
                    settle(pool)
                    flat = "p t d -> p (t d)"
                    wait(pool, summed, 3, it, s - 4)
                    settle(pool)
                    nc.gpsimd.tensor_scalar(u1[:], v1[:, :, par, :], alpha0, 1.0,
                                            ALU.mult, ALU.mult).then_inc(summed, 1)
                    nc.gpsimd.tensor_tensor(u23[:], u2[par][:], u3[par][:], ALU.add).then_inc(summed, 1)
                    pool.wait_ge(summed, it * (3 * BODY) + (3 * (s - 3) + 2))
                    settle(pool)
                    nc.gpsimd.tensor_tensor(res[:, bass.ds(it * BODY + (s - 3), 1), :, :].rearrange("p k t d -> p (k t d)"),
                                            u1[:].rearrange(flat), u23[:].rearrange(flat), ALU.add).then_inc(summed, 1)

            sweep(pool, slot)

            pool.wait_ge(xn_done, TILES)
            nc.gpsimd.tensor_tensor(x_sb[:], x_sb[:], bout[:].unsqueeze(1).to_broadcast([P, TILES, DIM]),
                                    ALU.add).then_inc(xb_done, 1)
            pool.wait_ge(summed, 3 * HEADS)

            def gather(b):
                for t in range(T):
                    reach(pool, rT_ready, (b - 1) * (2 * T) + (2 * t + 2))
                    nc.gpsimd.tensor_copy(rcur[t][:], res[:, bass.ds(b * H, H), t, :]).then_inc(rcur_done, 1)

            batches(pool, gather)

        @block.scalar
        def _(act):
            act.wait_ge(consts_in, 16 * CONSTS)
            nc.scalar.activation(late_sb[:, :, P:LATE], al_sb[:].rearrange("p (h c) -> p h c", h=NP), ACT.Exp,
                                 scale=-1.0).then_inc(alpha_exp, 1)
            act.wait_ge(dve_p, 2 * TILES + 1)
            nc.scalar.activation(std[:], mv[:, :, 1], ACT.Sqrt).then_inc(std_done, 1)
            for g in range(TILES // 4):
                act.wait_ge(xnT_ready, g + 1)
                nc.scalar.copy(xnT[:, g * 4 * P:(g + 1) * 4 * P], ps_x[g % 2][:]).then_inc(xnT_saved, 1)

            def slot(it, s):
                def alpha(j):
                    c = P + (s % 2) * ORDER + j
                    return late[((s - 2) // 2) % 2][:, c:c + 1]

                flat = "p t d -> p (t d)"
                def save_k(par, t, ranges):
                    for a, n, col in ranges:
                        nc.scalar.activation(k_sb[par][:, t, a:a + n], ps_qk[:, N + a:N + a + n], ACT.Identity,
                                             bias=cols[par][:, col:col + 1], scale=SCALE).then_inc(qk_saved, 1)

                def left_sum(t):
                    r, par = (s - 1) % BODY, (s - 1) % 2
                    a, n = ((0, MAXREL), (MAXREL, WIN))[t]
                    wait(act, left_done, T, it, s - 1)
                    wait(act, g_ready, 1, it, s - 1 - BODY)
                    nc.scalar.activation(lefts[par][:, a:a + n], lefts[par][:, a:a + n], ACT.Copy,
                                         accum_out=diag[r][:, t, 0:1]).then_inc(left_summed, 1)

                def save(ready, dst, col, t, saved):
                    act.wait_ge(ready, it * (T * BODY) + (T * (s - 2) + t + 1))
                    o = col + (s % 2) * DH
                    nc.scalar.copy(dst[:, t, s % 2, :], ps_r[:, t, o:o + DH]).then_inc(saved, 1)

                def exponent(t):
                    par = s % 2
                    wait(act, nmax_done, 1, it, s)
                    wait(act, masked, T, it, s - 2)
                    nc.scalar.activation(e_sb[par][:, t, :], s_sb[s % BODY][:, t, :], ACT.Exp,
                                         bias=nmax[par][:, t:t + 1], scale=1.0).then_inc(exp_done, 1)

                if there(it, s + 3):
                    r = (s + 3) % BODY
                    wait(act, p_ready, 1, it, s + 3)
                    wait_dma(act, band_out, it, s + 3 - BODY)
                    dst = bass.AP(band[r][:].tensor, EDGE0, [[T * EXT, P], [EXT + EDGE1 - EDGE0, T], [1, VOCAB]])
                    nc.scalar.copy(dst, ps_p[:, 0:T * VOCAB].rearrange("p (t c) -> p t c", t=T)).then_inc(band_saved, 1)
                if there(it, s - 2):
                    par = s % 2
                    wait(act, g_ready, 1, it, s - 2)
                    wait(act, r1_ready, T, it, s - 4)
                    nc.scalar.copy(diagT[par][:], ps_g[:, 0:N]).then_inc(g_saved, 1)
                if there(it, s):
                    exponent(0)
                if there(it, s):
                    exponent(1)
                if there(it, s - 2):
                    wait(act, summed, 3, it, s - 4)
                    for t in range(T):
                        save(r1_ready, v1, 0, t, r1_saved)
                if there(it, s + 3):
                    r = (s + 3) % BODY
                    for t, left_n in ((0, EDGE0), (1, EDGE1)):
                        o, c, right_n = t * EXT, t * VOCAB, EXT - VOCAB - left_n
                        nc.scalar.copy(band[r][:, o:o + left_n],
                                       ps_p[:, c:c + 1].to_broadcast([P, left_n])).then_inc(band_saved, 1)
                        nc.scalar.copy(band[r][:, o + left_n + VOCAB:o + EXT],
                                       ps_p[:, c + VOCAB - 1:c + VOCAB].to_broadcast([P, right_n])).then_inc(band_saved, 1)
                if there(it, s - 2):
                    save(r2_ready, v2, P, 0, r2_saved)
                if there(it, s - 1):
                    left_sum(0)
                if there(it, s - 2):
                    save(r2_ready, v2, P, 1, r2_saved)
                if there(it, s - 1):
                    left_sum(1)
                if there(it, s - 1):
                    par = (s - 1) % 2
                    wait(act, t_ready, 1, it, s - 1)
                    wait(act, r3_ready, T, it, s - 3)
                    nc.scalar.copy(aT[par][:].rearrange("p c n -> p (c n)"), ps_t[:]).then_inc(t_saved, 1)
                if there(it, s - 2):
                    par = s % 2
                    wait(act, r2_saved, T, it, s - 2)
                    nc.scalar.activation(u2[par][:], v2[:, :, par, :], ACT.Copy,
                                         scale=alpha(1)).then_inc(u_done, 1)
                if there(it, s - 2):
                    par = s % 2
                    if s % 2 == 0:
                        wait_pair_dma(act, late_in, 16, it, s - 2)
                    wait(act, r3_ready, T, it, s - 2)
                    nc.scalar.activation(u3[par][:], ps_r[:, :, 2 * P + par * DH:2 * P + (par + 1) * DH], ACT.Copy,
                                         scale=alpha(2)).then_inc(r3_saved, 1)
                if there(it, s + 2):
                    r = (s + 2) % BODY
                    wait(act, s_ready, 1, it, s + 2)
                    wait(act, masked, T, it, s + 2 - BODY)
                    nc.scalar.copy(s_sb[r][:].rearrange(flat), ps_s[:]).then_inc(s_saved, 1)
                if s % 2 == 1 and there(it, s + 3):
                    wait_pair(act, qk_ready, 1, it, s + 3)
                    save_k((s // 2) % 2, 1, ((0, N - WIN, 2), (N - WIN, WIN, 1)))
                if s % 2 == 0 and there(it, s + 4):
                    wait_pair(act, qk_ready, 1, it, s + 4)
                    wait(act, s_ready, 1, it, s + 1)
                    nc.scalar.activation(q_sb[(s // 2) % 2][:], ps_qk[:, 0:N], ACT.Identity, bias=cols[(s // 2) % 2][:, 0:1],
                                         scale=1.0).then_inc(qk_saved, 1)
                    save_k((s // 2) % 2, 0, ((0, WIN, 1), (WIN, N - WIN, 3)))
                if s % 2 == 1 and there(it, s + 1):
                    par = ((s + 1) // 2) % 2
                    wait_pair(act, v_ready, 1, it, s + 1)
                    wait(act, r1_ready, T, it, s - 2)
                    nc.scalar.copy(v_sb[par][:].rearrange("p t d -> p (t d)"), ps_v[:, 0:N]).then_inc(v_saved, 1)

            sweep(act, slot)

            def save_res(b):
                for t in range(T):
                    for half in range(2):
                        reach(act, y_ready, (b - 1) * T + (t + 1))
                        act.wait_ge(rT_ready, b * (2 * T) + (2 * t + half + 1))
                        nc.scalar.copy(rT[t][:, half * NP // 2:(half + 1) * NP // 2, :].rearrange("p h n -> p (h n)"),
                                       ps_x[half][:]).then_inc(rT_saved, 1)

            batches(act, save_res)
            act.wait_ge(y_stats, 1)
            nc.scalar.activation(std[:], mv[:, :, 1], ACT.Sqrt).then_inc(std2_done, 1)

            def second(b):
                for t in range(T):
                    act.wait_ge(ynT_ready, b * T + (t + 1))
                    nc.scalar.copy(ynT[t][:], ps_e[t][:, 0:P]).then_inc(ynT_saved, 1)
                    act.wait_ge(lmax_done, b * T + (t + 1))
                    nc.scalar.activation(gate[t][:], base[t][:, DIM:DIM + E_], ACT.Exp, bias=lmax[t][:, 0:1],
                                         scale=1.0, accum_out=gsum[t][:, 0:1]).then_inc(gate_exp, 1)
                    act.wait_ge(zT_ready, b * T + (t + 1))
                    nc.scalar.mul(zT[t][:], ps_e[t][0:E_ * R_, P:2 * P], SCALING).then_inc(zT_saved, 1)

            batches(act, second)

        @block.vector
        def _(dve):
            steps = [0]

            def own(ins):
                steps[0] += 1
                ins.then_inc(dve_p, 1)
                dve.wait_ge(dve_p, steps[0])

            dve.wait_ge(x_in, 16)
            for i in range(TILES):
                own(nc.vector.bn_stats(stats[:, i, :], x_sb[:, i, :]))
                own(nc.vector.bn_aggr(mv[:, i, :], stats[:, i, :]))
            own(nc.vector.tensor_scalar(mv[:, :, 1], mv[:, :, 1], EPS, None, ALU.add))
            dve.wait_ge(consts_in, 16 * CONSTS)
            own(nc.vector.tensor_tensor(relv[:], relv[:], relv0[:].unsqueeze(1).to_broadcast([P, 2, DH]), ALU.subtract))
            own(nc.vector.tensor_copy(colt[:, :, 0], bqk[:, :, 0]))
            own(nc.vector.tensor_scalar(colt[:, :, 1], bqk[:, :, 1], SCALE, None, ALU.mult))
            own(nc.vector.tensor_scalar(colt[:, :, 2], colt[:, :, 1], relk[:, 0:1], None, ALU.add))
            own(nc.vector.tensor_scalar(colt[:, :, 3], colt[:, :, 1], relk[:, VOCAB - 1:VOCAB], None, ALU.add))
            own(nc.vector.tensor_tensor(late_sb[:, :, 0:DH], bv_sb[:].rearrange("p (h c) -> p h c", h=NP)[:, :, 0:DH],
                                        relv0[0:1, :].unsqueeze(1).to_broadcast([1, NP, DH]), ALU.add))
            own(nc.vector.tensor_tensor(late_sb[:, :, DH:P], bv_sb[:].rearrange("p (h c) -> p h c", h=NP)[:, :, DH:P],
                                        relv0[0:1, :].unsqueeze(1).to_broadcast([1, NP, DH]), ALU.add))
            dve.wait_ge(alpha_exp, 1)
            own(nc.vector.tensor_scalar(late_sb[:, :, P:LATE], late_sb[:, :, P:LATE], 1.0, None, ALU.add))
            own(nc.vector.reciprocal(late_sb[:, :, P:LATE], late_sb[:, :, P:LATE]))
            for t in range(T):
                last = nc.vector.memset(z_sb[t][:], 0.0)
            last.then_inc(tables, 1)
            dve.wait_ge(std_done, 1)
            own(nc.vector.reciprocal(rstd[:], std[:]))
            for i in range(TILES):
                nc.vector.tensor_scalar(xn[:, i, :], x_sb[:, i, :], mv[:, i, 0:1], rstd[:, i:i + 1],
                                        ALU.subtract, ALU.mult).then_inc(xn_done, 1)

            STEPS = T * (2 * ROUNDS - 1)

            def divide(it, s):
                wait(dve, normed, T, it, s - 2)
                wait(dve, masked, T, it, s)
                nc.vector.reciprocal(rinv[s % 2][:], rsum[s % 2][:]).then_inc(rinv_done, 1)

            def slot(it, s):
                if there(it, s - 1) and not there(it, s):
                    divide(it, s - 1)
                if not there(it, s):
                    return
                par, r = s % 2, s % BODY
                m = top8[par]

                def own_step(i):
                    dve.wait_ge(top_step, i + 1)

                wait(dve, s_added, 1, it, s)
                settle(dve)
                if there(it, s - 1):
                    dve.wait_ge(top_step, STEPS)
                    dve.sem_clear(top_step)
                step = 0
                for n in range(ROUNDS):
                    for t in range(T):
                        src = s_sb[r][:, t, :] if n == 0 else work[t][:, (n - 1) % 2, :]
                        if n:
                            own_step(step - T)
                        nc.vector.max(m[:, t, 8 * n:8 * n + 8], src).then_inc(top_step, 1)
                        step += 1
                    if n == 0 and there(it, s - 1):
                        divide(it, s - 1)
                    if n < ROUNDS - 1:
                        for t in range(T):
                            src = s_sb[r][:, t, :] if n == 0 else work[t][:, (n - 1) % 2, :]
                            own_step(step - T)
                            nc.vector.match_replace(work[t][:, n % 2, :], m[:, t, 8 * n:8 * n + 8], src,
                                                    LOW).then_inc(top_step, 1)
                            step += 1
                    if n == 0:
                        wait(dve, exp_done, T, it, s - 2)
                        nc.vector.tensor_scalar(nmax[par][:], m[:, :, 0], -1.0, None, ALU.mult).then_inc(nmax_done, 1)
                wait(dve, exp_done, T, it, s)
                wait(dve, t_ready, 1, it, s - BODY)
                wait_dma(dve, diag_out, it, s - BODY)
                wait(dve, left_done, T, it, s - BODY)
                for t in range(T):
                    own_step(step - T + t)
                    nc.vector.scalar_tensor_tensor(a_sb[r][:, t, :], s_sb[r][:, t, :],
                                                   m[:, t, TOPK - 1:TOPK], e_sb[par][:, t, :], ALU.is_ge, ALU.mult,
                                                   accum_out=rsum[par][:, t:t + 1]).then_inc(masked, 1)

            sweep(dve, slot)

            dve.wait_ge(xb_done, 1)
            base_steps = steps[0]
            def add_attention(b):
                for t in range(T):
                    i = b * T + t
                    dve.wait_ge(y_ready, b * T + (t + 1))
                    y = y_sb[:, bass.ds(i, 1), :].rearrange("p i d -> p (i d)")
                    nc.vector.tensor_tensor(y, ps_y[t], y, ALU.add).then_inc(y_done, 1)
                    dve.wait_ge(y_done, b * T + (t + 1))
                    settle(dve)
                    nc.vector.bn_stats(stats[:, t, :], y).then_inc(dve_p, 1)
                    dve.wait_ge(dve_p, b * (3 * T) + (base_steps + 3 * t + 1))
                    settle(dve)
                    nc.vector.bn_aggr(agg[t][:], stats[:, t, :]).then_inc(dve_p, 1)
                    dve.wait_ge(dve_p, b * (3 * T) + (base_steps + 3 * t + 2))
                    settle(dve)
                    nc.vector.tensor_copy(mv[:, bass.ds(i, 1), :].rearrange("p i d -> p (i d)"), agg[t][:]).then_inc(dve_p, 1)
                    dve.wait_ge(dve_p, b * (3 * T) + (base_steps + 3 * t + 3))

            batches(dve, add_attention)
            nc.vector.tensor_scalar(mv[:, :, 1], mv[:, :, 1], EPS, None, ALU.add).then_inc(y_stats, 1)
            dve.wait_ge(std2_done, 1)
            base2 = base_steps + 3 * TILES
            nc.vector.reciprocal(rstd[:], std[:]).then_inc(dve_p, 1)
            dve.wait_ge(dve_p, base2 + 1)

            def second(b):
                for t in range(T):
                    i = b * T + t
                    k0 = base2 + 1 + 3 * t
                    y = y_sb[:, bass.ds(i, 1), :].rearrange("p i d -> p (i d)")
                    nc.vector.tensor_scalar(yn[t][:], y, mv[:, bass.ds(i, 1), 0:1].rearrange("p i d -> p (i d)"),
                                            rstd[:, bass.ds(i, 1)], ALU.subtract, ALU.mult).then_inc(yn_done, 1)
                    dve.wait_ge(f_ready, b * T + (t + 1))
                    nc.vector.tensor_tensor(base[t][:, 0:DIM + E_], ps_f[t][:, 0:DIM + E_], bffn[:],
                                            ALU.add).then_inc(dve_p, 1)
                    nc.vector.tensor_copy(base[t][:, DIM + E_:FFN], ps_f[t][:, DIM + E_:FFN]).then_inc(dve_p, 1)
                    dve.wait_ge(dve_p, b * (3 * T) + (k0 + 2))
                    nc.vector.tensor_reduce(lmax[t][:], base[t][:, DIM:DIM + E_], AX.X, ALU.max, negate=True).then_inc(lmax_done, 1)
                    dve.wait_ge(gate_exp, b * T + (t + 1))
                    nc.vector.reciprocal(gsum[t][:, 1:2], gsum[t][:, 0:1]).then_inc(dve_p, 1)
                    dve.wait_ge(dve_p, b * (3 * T) + (k0 + 3))
                    nc.vector.tensor_scalar(gbf[t][:], gate[t][:], gsum[t][:, 1:2], None, ALU.mult).then_inc(f_saved, 1)
                    dve.wait_ge(f_saved, b * T + (t + 1))
                    nc.vector.tensor_tensor(z_sb[t][:, 0:E_ * R_].rearrange("p (e r) -> p e r", e=E_), gbf[t][:].unsqueeze(2).to_broadcast([P, E_, R_]),
                                            base[t][:, DIM + E_:FFN].unsqueeze(1).to_broadcast([P, E_, R_]),
                                            ALU.mult).then_inc(z_done, 1)
                    dve.wait_ge(l_ready, b * T + (t + 1))
                    nc.vector.tensor_tensor(base[t][:, 0:DIM], base[t][:, 0:DIM], y, ALU.add).then_inc(y_done, 1)
                    dve.wait_ge(y_done, b * T + (TILES + t + 1))
                    reach(dve, out_sent[t], b * 16)
                    nc.vector.tensor_tensor(o_sb[t][:], ps_y[t], base[t][:, 0:DIM],
                                            ALU.add).then_inc(o_done, 1)

            batches(dve, second)

        @block.tensor
        def _(pe):
            mm, transpose = nc.tensor.matmul, nc.tensor.transpose
            pe.wait_ge(made, MADE)
            for g in range(TILES // 4):
                pe.wait_ge(xn_done, 4 * (g + 1))
                if g >= 2:
                    pe.wait_ge(xnT_saved, g - 1)
                for i in range(4):
                    last = transpose(ps_x[g % 2][:, i * P:(i + 1) * P], xn[:, 4 * g + i, :], ident[:])
                last.then_inc(xnT_ready, 1)
            pe.wait_ge(xnT_saved, TILES // 4)
            pe.wait_ge(tables, 1)

            def slot(it, s):
                def power(src, col, saved, ready):
                    par = s % 2
                    for t, c in ((0, 0), (0, 1), (1, 0), (1, 1)):
                        if t == 0:
                            reach_head(saved, s - 2, c)
                        last = mm(ps_r[:, t, col:col + P], aT[par][:, c, t * P:(t + 1) * P],
                                  src[:, c, :, :].rearrange("p h d -> p (h d)"), start=(c == 0), stop=(c == T - 1))
                        if c == T - 1:
                            last.then_inc(ready, 1)

                def reach_head(semaphore, j, c):
                    pe.wait_ge(semaphore, it * (T * BODY) + (T * j + c + 1))

                def scores(t):
                    j = s + 2
                    pair, h = (j // 2) % 2, (j % 2) * DH
                    return mm(ps_s[:, t * N:(t + 1) * N], q_sb[pair][h:h + DH, t * P:(t + 1) * P],
                              k_sb[pair][h:h + DH, t, :], start=True, stop=True)

                if there(it, s + 3):
                    j = s + 3
                    pair, h = (j // 2) % 2, (j % 2) * DH
                    wait_pair(pe, qk_saved, 5, it, j - 2)
                    pe.wait_ge(qk_saved, it * 10 + ((j // 2) * 5 + 1))
                    wait(pe, band_saved, 5, it, j - 1)
                    for t in range(T):
                        last = mm(ps_p[:, t * VOCAB:(t + 1) * VOCAB], q_sb[pair][h:h + DH, t * P:(t + 1) * P],
                                  relk[h:h + DH, :], start=True, stop=True)
                    last.then_inc(p_ready, 1)
                if there(it, s - 2):
                    r = (s - 2) % BODY
                    wait_dma(pe, diag_in, it, s - 2)
                    wait(pe, left_summed, T, it, s - 2)
                    wait(pe, g_saved, 1, it, s - 3)
                    for t in range(T):
                        last = transpose(ps_g[:, t * P:(t + 1) * P], diag[r][:, t, 0:P], ident[:])
                    last.then_inc(g_ready, 1)
                if there(it, s - 2):
                    j = s - 2
                    par, pair = j % 2, (j // 2) % 2
                    wait(pe, t_saved, 1, it, j)
                    wait_pair(pe, v_biased, 1, it, j)
                    wait(pe, r3_saved, 1, it, j - 1)
                    for t in range(T):
                        for c in range(T):
                            mm(ps_r[:, t, 0:P], aT[par][:, c, t * P:(t + 1) * P], v_sb[pair][:, c, :],
                               start=(c == 0), stop=False)
                if there(it, s - 2):
                    par = s % 2
                    wait(pe, g_saved, 1, it, s - 2)
                    for t in range(T):
                        mm(ps_r[:, t, 0:P], diagT[par][:, t * P:(t + 1) * P], relv[:].rearrange("p h d -> p (h d)"),
                           start=False, stop=True).then_inc(r1_ready, 1)
                if there(it, s + 2):
                    wait_pair(pe, qk_saved, 5, it, s + 2)
                    wait(pe, s_saved, 1, it, s + 1)
                    scores(0)
                if there(it, s - 2):
                    power(v1, P, r1_saved, r2_ready)
                if there(it, s - 1):
                    r, par = (s - 1) % BODY, (s - 1) % 2
                    wait(pe, normed, T, it, s - 1)
                    wait(pe, t_saved, 1, it, s - 2)
                    for c in range(T):
                        for t in range(T):
                            last = transpose(ps_t[:, c * N + t * P:c * N + (t + 1) * P],
                                             a_sb[r][:, t, c * P:(c + 1) * P], ident[:])
                    last.then_inc(t_ready, 1)
                if there(it, s - 2):
                    power(v2, 2 * P, r2_saved, r3_ready)
                if there(it, s + 2):
                    scores(1).then_inc(s_ready, 1)
                if s % 2 == 0 and there(it, s + 4):
                    pair = (s // 2) % 2
                    wait_pair_dma(pe, pair_in, 48, it, s + 4)
                    wait_pair(pe, qk_saved, 5, it, s + 2)
                    mm(ps_qk[:, 0:N], w_sb[pair][:, 0:P], xT[pair][:], start=True, stop=True)
                    mm(ps_qk[:, N:2 * N], w_sb[pair][:, P:2 * P], xT[pair][:], start=True,
                       stop=True).then_inc(qk_ready, 1)
                if s % 2 == 0 and there(it, s + 2):
                    pair = ((s + 2) // 2) % 2
                    wait_pair(pe, v_saved, 1, it, s)
                    for c in range(T):
                        last = mm(ps_v[:, c * P:(c + 1) * P], xT[pair][:, c * P:(c + 1) * P],
                                  w_sb[pair][:, 2 * P:3 * P], start=True, stop=True)
                    last.then_inc(v_ready, 1)

            sweep(pe, slot)

            pe.wait_ge(r3_saved, HEADS)
            pe.wait_ge(s_saved, HEADS)
            pe.wait_ge(qk_saved, 5 * HEADS // 2)
            def project(b):
                for t in range(T):
                    pe.wait_ge(rcur_done, b * T + (t + 1))
                    for half in range(2):
                        reach(pe, rT_saved, b * (2 * T) + (2 * t + half - 1))
                        for i in range(NP // 2):
                            h = half * NP // 2 + i
                            last = transpose(ps_x[half][:, i * P:(i + 1) * P],
                                             rcur[t][:, 2 * h:2 * h + 2, :].rearrange("p a d -> p (a d)"), ident[:])
                        last.then_inc(rT_ready, 1)
                    pe.wait_ge(rT_saved, b * (2 * T) + (2 * t + 2))
                    reach(pe, y_done, (b - 1) * T + (t + 1))
                    for h in range(NP):
                        last = mm(ps_y[t], rT[t][:, h, :], wout[:, h, :],
                                  start=(h == 0), stop=(h == NP - 1))
                    last.then_inc(y_ready, 1)

            batches(pe, project)
            pe.wait_ge(y_done, TILES)

            def second(b):
                for t in range(T):
                    pe.wait_ge(yn_done, b * T + (t + 1))
                    transpose(ps_e[t][:, 0:P], yn[t][:], ident[:]).then_inc(ynT_ready, 1)
                    pe.wait_ge(ynT_saved, b * T + (t + 1))
                    mm(ps_f[t][:, 0:FFN], ynT[t][:], wffn[:], start=True, stop=True).then_inc(f_ready, 1)
                    pe.wait_ge(z_done, b * T + (t + 1))
                    transpose(ps_e[t][:, P:2 * P], z_sb[t][:], ident[:]).then_inc(zT_ready, 1)
                    pe.wait_ge(zT_saved, b * T + (t + 1))
                    mm(ps_y[t], zT[t][:], lorab[:], start=True, stop=True).then_inc(l_ready, 1)

            batches(pe, second)


def kernel(L0_attn_x, L0_attn_Wqkv, L0_attn_bqkv, L0_attn_Wout, L0_attn_bout, L0_attn_rel_k_emb,
           L0_attn_rel_v_emb, L0_attn_alphas_raw, L0_ffn_base_w, L0_ffn_base_b, L0_ffn_lora_A, L0_ffn_lora_B,
           L0_ffn_router_w, L0_ffn_router_b):
    import concourse.bacc as bacc
    from concourse.bass_utils import run_bass_kernel_spmd

    f = {k: np.asarray(v) for k, v in dict(
        x=L0_attn_x, wqkv=L0_attn_Wqkv, bqkv=L0_attn_bqkv, wout=L0_attn_Wout, bout=L0_attn_bout,
        relk=L0_attn_rel_k_emb, relv=L0_attn_rel_v_emb, alphas=L0_attn_alphas_raw, bw=L0_ffn_base_w,
        bb=L0_ffn_base_b, la=L0_ffn_lora_A, lb=L0_ffn_lora_B, rw=L0_ffn_router_w, rb=L0_ffn_router_b).items()}
    inner, dim = f["wqkv"].shape[0] // 3, f["wqkv"].shape[1]
    pairs = inner // 128
    w = f["wqkv"].reshape(3, pairs, 128, dim).transpose(1, 3, 0, 2).reshape(pairs, dim, 3 * 128)
    bqk = f["bqkv"].reshape(3, pairs, 128)[:2].transpose(1, 2, 0)
    ins = {
        "x": f["x"],
        "wqkv": np.concatenate([w, bqk], axis=2),
        "bv": f["bqkv"][None, 2 * inner:],
        "wout": f["wout"].T,
        "bout": f["bout"][None, :],
        "relk": f["relk"][::-1].T,
        "relv": f["relv"][::-1],
        "alphas": f["alphas"].T.reshape(1, -1),
        "wffn": np.concatenate([f["bw"].T, f["rw"].T, f["la"]], axis=1),
        "bffn": np.concatenate([f["bb"], f["rb"]])[None, :],
        "lorab": f["lb"].reshape(-1, f["lb"].shape[2]),
    }
    nc = bacc.Bacc("TRN2", target_bir_lowering=False, num_devices=1)
    arrays, args = {}, []
    for name, a in ins.items():
        a = np.ascontiguousarray(a)
        arrays[f"in_{name}"] = a
        args.append(nc.dram_tensor(f"in_{name}", a.shape, mybir.dt.from_np(a.dtype), kind="ExternalInput").ap())
    args.append(nc.dram_tensor("out_0", f["x"].shape, mybir.dt.float32, kind="ExternalOutput").ap())
    preln_attention_ffn(nc, *args)
    r = run_bass_kernel_spmd(nc, [arrays], core_ids=[0])
    return r.results[0]["out_0"]
```

```python
import numpy as np
import concourse.bass as bass
from concourse import mybir
from contextlib import ExitStack


def preln_attention_ffn(nc: bass.Bass, x_d, wqkv_d, bv_d, wout_d, bout_d, relk_d, relv_d, alphas_d,
                        wffn_d, bffn_d, lorab_d, out_d):
    f32, bf16 = mybir.dt.float32, mybir.dt.bfloat16
    ALU, ACT = mybir.AluOpType, mybir.ActivationFunctionType
    AX = mybir.AxisListType

    B, N, DIM = x_d.shape
    P = 128
    DH = relv_d.shape[1]
    VOCAB = relv_d.shape[0]
    MAXREL = (VOCAB - 1) // 2
    NP = wqkv_d.shape[0]
    H = 2 * NP
    ORDER = alphas_d.shape[1] // H
    TOPK = 32
    ROUNDS = TOPK // 8
    SCALE = DH ** -0.5
    E_ = 8
    R_ = lorab_d.shape[0] // E_
    SCALING = 16 / R_
    EPS = 1e-5
    T = N // P
    TILES = B * T
    HEADS = B * H
    BODY = 4
    ITS = HEADS // BODY
    LOW = -3.0e38
    WIN = 192
    EXT = 2 * P + MAXREL - 1
    EDGE0, EDGE1 = MAXREL - 1, P - 1
    FFN = DIM + E_ + R_
    LATE = P + 2 * ORDER

    xT_d = nc.dram_tensor("xT_scratch", (P, B * N), f32).ap()
    cols_d = nc.dram_tensor("cols_scratch", (P, NP * 4), f32).ap()
    late_d = nc.dram_tensor("late_scratch", (NP, LATE), f32).ap()
    band_d = [nc.dram_tensor(f"band_scratch{i}", (P, T * EXT), f32).ap() for i in range(BODY)]
    diag_d = [nc.dram_tensor(f"diag_scratch{i}", (P, T * 2 * P), f32).ap() for i in range(BODY)]

    ctx = ExitStack()
    with ctx:
        def sb(name, shape, dt=f32):
            return ctx.enter_context(nc.sbuf_tensor(name, shape, dt))

        def sem(name):
            return ctx.enter_context(nc.semaphore(name))

        ident = sb("ident", [P, P])
        ones = sb("ones", [P, WIN])
        left = sb("left", [P, MAXREL + WIN])
        relk = sb("relk", [P, VOCAB])
        relv = sb("relv", [P, 2, DH])
        relv0 = sb("relv0", [P, DH])
        colt = sb("colt", [P, NP, 4])
        bqk = sb("bqk", [P, NP, 2])
        late_sb = sb("late_sb", [1, NP, LATE])
        bv_sb = sb("bv_sb", [1, NP * P])
        al_sb = sb("al_sb", [1, NP * 2 * ORDER])
        zeros = sb("zeros", [P, 2 * P * T])
        x_sb = sb("x_sb", [P, TILES, DIM])
        stats = sb("stats", [P, TILES, 6])
        mv = sb("mv", [P, TILES, 2])
        std = sb("std", [P, TILES])
        rstd = sb("rstd", [P, TILES])
        xn = sb("xn", [P, TILES, DIM])
        xnT = sb("xnT", [P, B * N])
        w_sb = [sb(f"w_sb{i}", [P, 3 * P]) for i in range(2)]
        xT = [sb(f"xT{i}", [P, N]) for i in range(2)]
        cols = [sb(f"cols{i}", [P, 4]) for i in range(2)]
        late = [sb(f"late{i}", [P, LATE]) for i in range(2)]
        q_sb = [sb(f"q_sb{i}", [P, N]) for i in range(2)]
        k_sb = [sb(f"k_sb{i}", [P, T, N]) for i in range(2)]
        v_sb = [sb(f"v_sb{i}", [P, T, P]) for i in range(2)]
        band = [sb(f"band{i}", [P, T * EXT]) for i in range(BODY)]
        skew = [sb(f"skew{i}", [P, T, N]) for i in range(BODY)]
        s_sb = [sb(f"s_sb{i}", [P, T, N]) for i in range(BODY)]
        top8 = [sb(f"top8_{i}", [P, T, ROUNDS * 8]) for i in range(2)]
        work = [sb(f"work{t}", [P, 2, N]) for t in range(T)]
        nmax = [sb(f"nmax{i}", [P, T]) for i in range(2)]
        rsum = [sb(f"rsum{i}", [P, T]) for i in range(2)]
        rinv = [sb(f"rinv{i}", [P, T]) for i in range(2)]
        e_sb = [sb(f"e_sb{i}", [P, T, N]) for i in range(2)]
        a_sb = [sb(f"a_sb{i}", [P, T, N]) for i in range(BODY)]
        aT = [sb(f"aT{i}", [P, T, N]) for i in range(2)]
        lefts = [sb(f"lefts{i}", [P, MAXREL + WIN]) for i in range(2)]
        diag = [sb(f"diag{i}", [P, T, P + 1]) for i in range(BODY)]
        diagT = [sb(f"diagT{i}", [P, N]) for i in range(2)]
        v1 = sb("v1", [P, T, 2, DH])
        v2 = sb("v2", [P, T, 2, DH])
        u1 = sb("u1", [P, T, DH])
        u2 = sb("u2", [P, T, DH])
        u3 = [sb(f"u3_{i}", [P, T, DH]) for i in range(2)]
        u23 = sb("u23", [P, T, DH])
        res = sb("res", [P, HEADS, T, DH])
        wout = sb("wout", [P, NP, DIM])
        bout = sb("bout", [P, DIM])
        wffn = sb("wffn", [P, FFN])
        bffn = sb("bffn", [P, FFN])
        lorab = sb("lorab", [P, DIM])
        rcur = [sb(f"rcur{t}", [P, H, DH]) for t in range(T)]
        rT = [sb(f"rT{t}", [P, NP, P]) for t in range(T)]
        y_sb, yn, ynT, o_sb, zT = x_sb, xn, xnT, xn, rT[0]
        z_sb = rcur[0][:].rearrange("p h (a r) -> p (h a) r", r=R_).rearrange("p (i e) r -> p i e r", e=E_)
        ffn = res[:, 0:TILES * FFN // (T * DH), :, :].rearrange("p k t d -> p (k t d)").rearrange("p (i c) -> p i c", c=FFN)
        lmax = sb("lmax", [P, TILES])
        gate = sb("gate", [P, TILES, E_])
        gsum = sb("gsum", [P, TILES])
        ginv = sb("ginv", [P, TILES])
        gbf = sb("gbf", [P, TILES, E_], bf16)

        def pb(name):
            return ctx.enter_context(nc.psum_tensor(name, [P, 512], f32))

        ps_s, ps_t, ps_g, ps_qk, ps_p, ps_v = (pb(n) for n in ("ps_s", "ps_t", "ps_g", "ps_qk", "ps_p", "ps_v"))
        ps_r = ctx.enter_context(nc.psum_tensor("ps_r", [P, T, 512], f32))

        ps_x, ps_f = [ps_s, ps_qk], [ps_p, ps_v]
        ps_y = [ps_r[:, t, 0:DIM] for t in range(T)]
        ps_l = [ps_r[:, 0, :], ps_r[:, 1, :], ps_t[:], ps_g[:]]

        consts_in = sem("consts_in")
        x_in = sem("x_in")
        made = sem("made")
        scratch_zero = sem("scratch_zero")
        tables = sem("tables")
        alpha_exp = sem("alpha_exp")
        tables_out = sem("tables_out")
        dve_p = sem("dve_p")
        std_done = sem("std_done")
        xn_done = sem("xn_done")
        xnT_ready = sem("xnT_ready")
        xnT_saved = sem("xnT_saved")
        xT_out = sem("xT_out")
        pair_in = [sem("pair_in0"), sem("pair_in1")]
        late_in = [sem("late_in0"), sem("late_in1")]
        qk_ready, qk_saved = sem("qk_ready"), sem("qk_saved")
        v_ready, v_saved, v_biased = sem("v_ready"), sem("v_saved"), sem("v_biased")
        p_ready, band_saved = sem("p_ready"), sem("band_saved")
        band_out = [sem(f"band_out{i}") for i in range(BODY)]
        skew_in = [sem(f"skew_in{i}") for i in range(BODY)]
        s_ready, s_saved = sem("s_ready"), sem("s_saved")
        s_added = sem("s_added")
        top_step = sem("top_step")
        nmax_done, exp_done = sem("nmax_done"), sem("exp_done")
        masked, rinv_done = sem("masked"), sem("rinv_done")
        normed = sem("normed")
        diag_out = [sem(f"diag_out{i}") for i in range(BODY)]
        diag_in = [sem(f"diag_in{i}") for i in range(BODY)]
        t_ready, t_saved = sem("t_ready"), sem("t_saved")
        g_ready, g_saved = sem("g_ready"), sem("g_saved")
        left_done, left_summed = sem("left_done"), sem("left_summed")
        r1_ready, r2_ready, r3_ready = sem("r1_ready"), sem("r2_ready"), sem("r3_ready")
        r1_saved, r2_saved, r3_saved = sem("r1_saved"), sem("r2_saved"), sem("r3_saved")
        summed = sem("summed")
        passed = sem("passed")
        xb_done = sem("xb_done")
        rcur_done = sem("rcur_done")
        rT_ready, rT_saved = sem("rT_ready"), sem("rT_saved")
        y_ready, y_done = sem("y_ready"), sem("y_done")
        y_stats = sem("y_stats")
        std2_done = sem("std2_done")
        yn_done, ynT_ready, ynT_saved = sem("yn_done"), sem("ynT_ready"), sem("ynT_saved")
        f_ready, f_saved = sem("f_ready"), sem("f_saved")
        lmax_done, gate_exp = sem("lmax_done"), sem("gate_exp")
        z_done, zT_ready, zT_saved = sem("z_done"), sem("zT_ready"), sem("zT_saved")
        l_ready, o_done = sem("l_ready"), sem("o_done")
        row_stats = sem("row_stats")
        by_done = sem("by_done")
        out_sent = sem("out_sent")

        block = ctx.enter_context(nc.Block())

        def sweep(eng, slot):
            for it in (-1, 0, 1):
                for s in range(BODY):
                    slot(it, s)
            with eng.Fori(2, ITS - 2) as it:
                for s in range(BODY):
                    slot(it, s)
            for it in (ITS - 2, ITS - 1, ITS):
                for s in range(BODY):
                    slot(it, s)

        def there(it, s):
            return not isinstance(it, int) or 0 <= BODY * it + s < HEADS

        def wait(eng, semaphore, each, it, s):
            if not isinstance(it, int) or BODY * it + s >= 0:
                eng.wait_ge(semaphore, it * (BODY * each) + (s + 1) * each)

        def wait_pair(eng, semaphore, each, it, s):
            if not isinstance(it, int) or BODY * it + s >= 0:
                eng.wait_ge(semaphore, it * (2 * each) + (s // 2 + 1) * each)

        def wait_dma(eng, ring, it, s):
            if not isinstance(it, int) or BODY * it + s >= 0:
                eng.wait_ge(ring[s % BODY], it * 16 + (s // BODY + 1) * 16)

        def wait_pair_dma(eng, ring, each, it, s):
            if not isinstance(it, int) or BODY * it + s >= 0:
                p = s // 2
                eng.wait_ge(ring[p % 2], it * each + (p // 2 + 1) * each)

        def batches(eng, body):
            body(0)
            with eng.Fori(1, B) as b:
                body(b)

        def reach(eng, semaphore, value):
            if not isinstance(value, int) or value > 0:
                eng.wait_ge(semaphore, value)

        def settle(eng):
            eng.sem_inc(passed)

        CONSTS = 14
        MADE = 8 + BODY

        @block.sync
        def _(sp):
            sp.dma_start(x_sb[:], x_d.rearrange("b (t p) d -> p (b t) d", p=P)).then_inc(x_in, 16)
            for dst, src in ((relk[0:DH, :], relk_d), (relk[DH:P, :], relk_d), (relv[:, 0, :], relv_d[0:P, :]), (relv[:, 1, :], relv_d[0:P, :]),
                             (relv0[:], relv_d[P:P + 1, :].to_broadcast([P, DH])),
                             (bqk[:], wqkv_d[:, :, 3 * P:3 * P + 2].rearrange("h p c -> p h c")),
                             (bv_sb[:], bv_d), (al_sb[:], alphas_d),
                             (wout[:], wout_d.rearrange("(h p) n -> p h n", p=P)),
                             (bout[:], bout_d.to_broadcast([P, DIM])), (wffn[:], wffn_d),
                             (bffn[:, 0:DIM + E_], bffn_d.to_broadcast([P, DIM + E_])),
                             (lorab[0:E_ * R_, :], lorab_d), (lorab[E_ * R_:P, :], lorab_d)):
                sp.dma_start(dst, src).then_inc(consts_in, 16)
            sp.wait_ge(made, MADE)
            for i in range(BODY):
                sp.dma_start(diag_d[i], zeros[:]).then_inc(scratch_zero, 16)
            G = B * N // (TILES // 4)
            sp.wait_ge(xnT_saved, 1)
            sp.dma_start(xT_d[:, 0:G], xnT[:, 0:G]).then_inc(xT_out, 16)
            sp.wait_ge(tables, 1)
            sp.dma_start(cols_d, colt[:].rearrange("p h c -> p (h c)")).then_inc(tables_out, 16)
            sp.dma_start(late_d.rearrange("h c -> (h c)").unsqueeze(0), late_sb[:].rearrange("p h c -> p (h c)")).then_inc(tables_out, 16)
            sp.wait_ge(xT_out, 16)
            sp.wait_ge(tables_out, 32)
            sp.wait_ge(scratch_zero, 16 * BODY)

            def load_pair(it, s):
                par = (s // 2) % 2
                pair = it * 2 + s // 2
                hp, b = pair % NP, pair // NP
                wait_pair(sp, v_ready, 1, it, s - 4)
                settle(sp)
                wait_pair(sp, qk_saved, 4, it, s - 4)
                settle(sp)
                sp.dma_start(w_sb[par][:], wqkv_d[bass.ds(hp, 1), :, 0:3 * P].rearrange("h p c -> p (h c)")
                             ).then_inc(pair_in[par], 16)
                sp.dma_start(cols[par][:], cols_d[:, bass.ds(hp * 4, 4)]).then_inc(pair_in[par], 16)
                sp.dma_start(xT[par][:], xT_d[:, bass.ds(b * N, N)]).then_inc(pair_in[par], 16)

            def load_late(it, s):
                par = (s // 2) % 2
                hp = (it * 2 + s // 2) % NP
                wait_pair(sp, v_biased, 1, it, s - 4)
                settle(sp)
                wait(sp, r3_saved, 1, it, s - 3)
                settle(sp)
                wait(sp, summed, 4, it, s - 3)
                settle(sp)
                sp.dma_start(late[par][:], late_d[bass.ds(hp, 1), :].to_broadcast([P, LATE])
                             ).then_inc(late_in[par], 16)

            load_pair(0, 0)
            sp.wait_ge(xnT_saved, TILES // 4)
            sp.dma_start(xT_d[:, G:B * N], xnT[:, G:B * N]).then_inc(xT_out, 16)
            sp.wait_ge(xT_out, 32)

            def slot(it, s):
                if there(it, s - 1):
                    r = (s - 1) % BODY
                    wait(sp, normed, T, it, s - 1)
                    settle(sp)
                    wait_dma(sp, diag_in, it, s - 1 - BODY)
                    src = a_sb[r][:].rearrange("p t n -> p (t n)")
                    src = bass.AP(src.tensor, 0, [[T * N, P], [N + MAXREL, T], [1, WIN]])
                    dst = bass.AP(diag_d[r].tensor, MAXREL, [[T * 2 * P, P], [WIN, T], [1, WIN]])
                    sp.dma_start(dst, src).then_inc(diag_out[r], 16)
                if s % 2 == 1 and there(it, s + 5):
                    load_pair(it, s + 5)
                if there(it, s - 1):
                    r = (s - 1) % BODY
                    wait_dma(sp, diag_out, it, s - 1)
                    settle(sp)
                    wait(sp, g_ready, 1, it, s - 1 - BODY)
                    src = bass.AP(diag_d[r].tensor, 1, [[T * 2 * P + 1, P], [2 * P, T], [1, P]])
                    sp.dma_start(diag[r][:, :, 1:P + 1], src).then_inc(diag_in[r], 16)
                if there(it, s + 2):
                    r = (s + 2) % BODY
                    wait_dma(sp, band_out, it, s + 2)
                    settle(sp)
                    wait(sp, s_added, 1, it, s + 2 - BODY)
                    src = bass.AP(band_d[r].tensor, P - 1, [[T * EXT - 1, P], [EXT, T], [1, WIN]])
                    dst = bass.AP(skew[r][:].tensor, 0, [[T * N, P], [N + MAXREL, T], [1, WIN]])
                    sp.dma_start(dst, src).then_inc(skew_in[r], 16)
                if there(it, s + 3):
                    r = (s + 3) % BODY
                    wait(sp, band_saved, 3, it, s + 3)
                    settle(sp)
                    wait_dma(sp, skew_in, it, s + 3 - BODY)
                    sp.dma_start(band_d[r], band[r][:]).then_inc(band_out[r], 16)
                if s % 2 == 0 and there(it, s):
                    load_late(it, s)

            sweep(sp, slot)

            for h in range(2):
                sp.wait_ge(o_done, T * (h + 1))
                sp.dma_start(out_d[h * B // 2:(h + 1) * B // 2].rearrange("b (t p) d -> p (b t) d", p=P),
                             o_sb[:, h * TILES // 2:(h + 1) * TILES // 2, :]).then_inc(out_sent, 16)
            sp.wait_ge(out_sent, 32)

        @block.gpsimd
        def _(pool):
            nc.gpsimd.memset(ones[:], 1.0).then_inc(made, 1)
            pool.wait_ge(made, 1)
            nc.gpsimd.affine_select(out=ident[:], in_=ones[:, 0:P], compare_op=ALU.is_equal, fill=0.0, base=0,
                                    pattern=[[-1, P]], channel_multiplier=1).then_inc(made, 1)
            for a, n, base in ((0, MAXREL, -MAXREL), (MAXREL, WIN, P - MAXREL)):
                nc.gpsimd.affine_select(out=left[:, a:a + n], in_=ones[:, 0:n], compare_op=ALU.is_ge, fill=0.0,
                                        base=base, pattern=[[-1, n]], channel_multiplier=1).then_inc(made, 1)
            nc.gpsimd.memset(bffn[:, DIM + E_:FFN], 0.0).then_inc(made, 1)
            nc.gpsimd.memset(v1[:], 0.0).then_inc(made, 1)
            nc.gpsimd.memset(v2[:], 0.0).then_inc(made, 1)
            for i in range(BODY):
                nc.gpsimd.memset(skew[i][:], 0.0).then_inc(made, 1)
            nc.gpsimd.memset(zeros[:], 0.0).then_inc(made, 1)
            pool.wait_ge(x_in, 16)
            pool.wait_ge(consts_in, 16 * CONSTS)
            pool.wait_ge(made, MADE)

            pool.wait_ge(xn_done, TILES)
            nc.gpsimd.tensor_tensor(x_sb[:], x_sb[:], bout[:].unsqueeze(1).to_broadcast([P, TILES, DIM]),
                                    ALU.add).then_inc(xb_done, 1)
            def slot(it, s):
                if there(it, s - 1):
                    r, par = (s - 1) % BODY, (s - 1) % 2
                    wait(pool, rinv_done, 1, it, s - 1)
                    settle(pool)
                    for t in range(T):
                        nc.gpsimd.tensor_scalar(a_sb[r][:, t, :], a_sb[r][:, t, :], rinv[par][:, t:t + 1], 1.0,
                                                ALU.mult, ALU.mult).then_inc(normed, 1)
                if there(it, s - 1):
                    r, par = (s - 1) % BODY, (s - 1) % 2
                    wait(pool, left_summed, T, it, s - 3)
                    wait(pool, normed, T, it, s - 1)
                    nc.gpsimd.tensor_tensor(lefts[par][:, 0:MAXREL], a_sb[r][:, 0, 0:MAXREL], left[:, 0:MAXREL],
                                            ALU.mult).then_inc(left_done, 1)
                    nc.gpsimd.tensor_tensor(lefts[par][:, MAXREL:MAXREL + WIN], a_sb[r][:, 1, 0:WIN],
                                            left[:, MAXREL:MAXREL + WIN], ALU.mult).then_inc(left_done, 1)
                if there(it, s + 1):
                    r = (s + 1) % BODY
                    wait_dma(pool, skew_in, it, s + 1)
                    wait(pool, s_saved, 1, it, s + 1)
                    nc.gpsimd.tensor_tensor(s_sb[r][:], s_sb[r][:], skew[r][:], ALU.add).then_inc(s_added, 1)
                if s % 2 == 1 and there(it, s - 1):
                    par = ((s - 1) // 2) % 2
                    wait_pair(pool, v_saved, 1, it, s - 1)
                    wait_pair_dma(pool, late_in, 16, it, s - 1)
                    nc.gpsimd.tensor_tensor(v_sb[par][:], v_sb[par][:],
                                            late[par][:, 0:P].unsqueeze(1).to_broadcast([P, T, P]),
                                            ALU.add).then_inc(v_biased, 1)
                if there(it, s - 3):
                    par = (s - 3) % 2
                    c = P + ((s - 3) % 2) * ORDER
                    alpha = late[((s - 3) // 2) % 2]
                    wait_pair_dma(pool, late_in, 16, it, s - 3)
                    wait(pool, r3_saved, 1, it, s - 3)
                    settle(pool)
                    flat = "p t d -> p (t d)"
                    wait(pool, summed, 4, it, s - 4)
                    settle(pool)
                    for u, v, i in ((u1, v1, c), (u2, v2, c + 1)):
                        nc.gpsimd.tensor_scalar(u[:], v[:, :, par, :], alpha[:, i:i + 1], 1.0,
                                                ALU.mult, ALU.mult).then_inc(summed, 1)
                    pool.wait_ge(summed, it * (4 * BODY) + (4 * (s - 3) + 2))
                    settle(pool)
                    nc.gpsimd.tensor_tensor(u23[:], u2[:], u3[par][:], ALU.add).then_inc(summed, 1)
                    pool.wait_ge(summed, it * (4 * BODY) + (4 * (s - 3) + 3))
                    settle(pool)
                    nc.gpsimd.tensor_tensor(res[:, bass.ds(it * BODY + (s - 3), 1), :, :].rearrange("p k t d -> p (k t d)"),
                                            u1[:].rearrange(flat), u23[:].rearrange(flat), ALU.add).then_inc(summed, 1)

            sweep(pool, slot)

            for g in range(TILES // 4):
                pool.wait_ge(f_saved, 2 * g + 2)
                pool.wait_ge(y_done, TILES)
                nc.gpsimd.tensor_tensor(y_sb[:, 4 * g:4 * g + 4, :], y_sb[:, 4 * g:4 * g + 4, :],
                                        ffn[:, 4 * g:4 * g + 4, 0:DIM], ALU.add).then_inc(by_done, 1)

        @block.scalar
        def _(act):
            act.wait_ge(row_stats, 2 * TILES + 1)
            nc.scalar.activation(std[:], mv[:, :, 1], ACT.Sqrt).then_inc(std_done, 1)
            act.wait_ge(consts_in, 16 * CONSTS)
            nc.scalar.activation(late_sb[:, :, P:LATE], al_sb[:].rearrange("p (h c) -> p h c", h=NP), ACT.Exp,
                                 scale=-1.0).then_inc(alpha_exp, 1)
            for g in range(TILES // 4):
                act.wait_ge(xnT_ready, g + 1)
                nc.scalar.copy(xnT[:, g * 4 * P:(g + 1) * 4 * P], ps_x[g % 2][:]).then_inc(xnT_saved, 1)

            def slot(it, s):
                def alpha(j):
                    c = P + (s % 2) * ORDER + j
                    return late[((s - 2) // 2) % 2][:, c:c + 1]

                flat = "p t d -> p (t d)"
                def left_sum(t):
                    r, par = (s - 1) % BODY, (s - 1) % 2
                    a, n = ((0, MAXREL), (MAXREL, WIN))[t]
                    wait(act, left_done, T, it, s - 1)
                    wait(act, g_ready, 1, it, s - 1 - BODY)
                    nc.scalar.activation(lefts[par][:, a:a + n], lefts[par][:, a:a + n], ACT.Copy,
                                         accum_out=diag[r][:, t, 0:1]).then_inc(left_summed, 1)

                def save(ready, dst, col, t, saved):
                    act.wait_ge(ready, it * (T * BODY) + (T * (s - 2) + t + 1))
                    o = col + (s % 2) * DH
                    nc.scalar.copy(dst[:, t, s % 2, :], ps_r[:, t, o:o + DH]).then_inc(saved, 1)

                def exponent(t):
                    par = s % 2
                    wait(act, nmax_done, 1, it, s)
                    wait(act, masked, T, it, s - 2)
                    nc.scalar.activation(e_sb[par][:, t, :], s_sb[s % BODY][:, t, :], ACT.Exp,
                                         bias=nmax[par][:, t:t + 1], scale=1.0).then_inc(exp_done, 1)

                if there(it, s):
                    exponent(1)
                if there(it, s - 2):
                    par = s % 2
                    wait(act, g_ready, 1, it, s - 2)
                    wait(act, r1_ready, T, it, s - 4)
                    nc.scalar.copy(diagT[par][:], ps_g[:, 0:N]).then_inc(g_saved, 1)
                if there(it, s + 3):
                    r = (s + 3) % BODY
                    wait(act, p_ready, 1, it, s + 3)
                    wait_dma(act, band_out, it, s + 3 - BODY)
                    dst = bass.AP(band[r][:].tensor, EDGE0, [[T * EXT, P], [EXT + EDGE1 - EDGE0, T], [1, VOCAB]])
                    nc.scalar.copy(dst, ps_p[:, 0:T * VOCAB].rearrange("p (t c) -> p t c", t=T)).then_inc(band_saved, 1)
                if there(it, s):
                    exponent(0)
                if there(it, s - 2):
                    wait(act, summed, 4, it, s - 4)
                    for t in range(T):
                        save(r1_ready, v1, 0, t, r1_saved)
                if there(it, s + 3):
                    r = (s + 3) % BODY
                    nc.scalar.copy(band[r][:, EDGE0 + VOCAB:EXT + EDGE1].rearrange("p (t c) -> p t c", t=T),
                                   ps_p[:, VOCAB - 1:VOCAB + 1].unsqueeze(2).to_broadcast([P, T, EDGE1])
                                   ).then_inc(band_saved, 1)
                    dst = bass.AP(band[r][:].tensor, 0, [[T * EXT, P], [EXT + EDGE1 + VOCAB, T], [1, EDGE0]])
                    nc.scalar.copy(dst, ps_p[:, 0:T * VOCAB:T * VOCAB - 1].unsqueeze(2).to_broadcast([P, T, EDGE0])
                                   ).then_inc(band_saved, 1)
                if there(it, s - 2):
                    save(r2_ready, v2, P, 0, r2_saved)
                if there(it, s - 1):
                    left_sum(0)
                if there(it, s - 2):
                    save(r2_ready, v2, P, 1, r2_saved)
                if there(it, s - 1):
                    left_sum(1)
                if there(it, s - 1):
                    par = (s - 1) % 2
                    wait(act, t_ready, 1, it, s - 1)
                    wait(act, r3_ready, T, it, s - 3)
                    nc.scalar.copy(aT[par][:].rearrange("p c n -> p (c n)"), ps_t[:]).then_inc(t_saved, 1)
                if s % 2 == 1 and there(it, s + 3):
                    wait_pair(act, qk_ready, 1, it, s + 3)
                    par = (s // 2) % 2
                    for t, a, col in ((0, WIN, 3), (1, 0, 2)):
                        nc.scalar.activation(k_sb[par][:, t, a:a + N - WIN], ps_qk[:, N + a:N + a + N - WIN],
                                             ACT.Identity, bias=cols[par][:, col:col + 1],
                                             scale=SCALE).then_inc(qk_saved, 1)
                if there(it, s - 2):
                    par = s % 2
                    if s % 2 == 0:
                        wait_pair_dma(act, late_in, 16, it, s - 2)
                    wait(act, r3_ready, T, it, s - 2)
                    nc.scalar.activation(u3[par][:], ps_r[:, :, 2 * P + par * DH:2 * P + (par + 1) * DH], ACT.Copy,
                                         scale=alpha(2)).then_inc(r3_saved, 1)
                if s % 2 == 0 and there(it, s + 4):
                    wait_pair(act, qk_ready, 1, it, s + 4)
                    wait(act, s_ready, 1, it, s + 1)
                    par = (s // 2) % 2
                    nc.scalar.activation(q_sb[par][:], ps_qk[:, 0:N], ACT.Identity, bias=cols[par][:, 0:1],
                                         scale=1.0).then_inc(qk_saved, 1)
                    dst = bass.AP(k_sb[par][:].tensor, 0, [[T * N, P], [N + MAXREL, T], [1, WIN]])
                    src = bass.AP(ps_qk[:].tensor, N, [[512, P], [MAXREL, T], [1, WIN]])
                    nc.scalar.activation(dst, src, ACT.Identity, bias=cols[par][:, 1:2],
                                         scale=SCALE).then_inc(qk_saved, 1)
                if s % 2 == 1 and there(it, s + 1):
                    par = ((s + 1) // 2) % 2
                    wait_pair(act, v_ready, 1, it, s + 1)
                    wait(act, r1_ready, T, it, s - 2)
                    nc.scalar.copy(v_sb[par][:].rearrange("p t d -> p (t d)"), ps_v[:, 0:N]).then_inc(v_saved, 1)
                if there(it, s + 2):
                    r = (s + 2) % BODY
                    wait(act, s_ready, 1, it, s + 2)
                    wait(act, masked, T, it, s + 2 - BODY)
                    nc.scalar.copy(s_sb[r][:].rearrange(flat), ps_s[:]).then_inc(s_saved, 1)

            sweep(act, slot)

            def save_res(b):
                for t in range(T):
                    for half in range(2):
                        reach(act, y_ready, (b - 1) * T + (t + 1))
                        act.wait_ge(rT_ready, b * (2 * T) + (2 * t + half + 1))
                        nc.scalar.copy(rT[t][:, half * NP // 2:(half + 1) * NP // 2, :].rearrange("p h n -> p (h n)"),
                                       ps_x[half][:]).then_inc(rT_saved, 1)

            batches(act, save_res)
            act.wait_ge(y_stats, 1)
            nc.scalar.activation(std[:], mv[:, :, 1], ACT.Sqrt).then_inc(std2_done, 1)
            for g in range(TILES // 4):
                act.wait_ge(ynT_ready, g + 1)
                nc.scalar.copy(ynT[:, g * 4 * P:(g + 1) * 4 * P], ps_x[g % 2][:]).then_inc(ynT_saved, 1)
            for h in range(2):
                a = h * TILES // 2
                act.wait_ge(lmax_done, h + 1)
                nc.scalar.activation(gate[:, a:a + TILES // 2, :], gate[:, a:a + TILES // 2, :],
                                     ACT.Exp).then_inc(gate_exp, 1)
            for h in range(2):
                act.wait_ge(zT_ready, h + 1)
                nc.scalar.mul(zT[:, h * B // 2:(h + 1) * B // 2, :].rearrange("p b n -> p (b n)"), ps_x[h][:],
                              SCALING).then_inc(zT_saved, 1)

        @block.vector
        def _(dve):
            steps = [0]

            def own(ins):
                steps[0] += 1
                ins.then_inc(dve_p, 1)
                dve.wait_ge(dve_p, steps[0])

            dve.wait_ge(x_in, 16)
            for i in range(TILES):
                nc.vector.bn_stats(stats[:, i, :], x_sb[:, i, :]).then_inc(row_stats, 1)
            dve.wait_ge(row_stats, TILES)
            for i in range(TILES):
                nc.vector.bn_aggr(mv[:, i, :], stats[:, i, :]).then_inc(row_stats, 1)
            dve.wait_ge(row_stats, 2 * TILES)
            nc.vector.tensor_scalar(mv[:, :, 1], mv[:, :, 1], EPS, None, ALU.add).then_inc(row_stats, 1)
            dve.wait_ge(std_done, 1)
            own(nc.vector.reciprocal(rstd[:], std[:]))
            for i in range(TILES):
                nc.vector.tensor_scalar(xn[:, i, :], x_sb[:, i, :], mv[:, i, 0:1], rstd[:, i:i + 1],
                                        ALU.subtract, ALU.mult).then_inc(xn_done, 1)
            dve.wait_ge(consts_in, 16 * CONSTS)
            own(nc.vector.tensor_tensor(relv[:], relv[:], relv0[:].unsqueeze(1).to_broadcast([P, 2, DH]), ALU.subtract))
            own(nc.vector.tensor_copy(colt[:, :, 0], bqk[:, :, 0]))
            own(nc.vector.tensor_scalar(colt[:, :, 1], bqk[:, :, 1], SCALE, None, ALU.mult))
            own(nc.vector.tensor_scalar(colt[:, :, 2], colt[:, :, 1], relk[:, 0:1], None, ALU.add))
            own(nc.vector.tensor_scalar(colt[:, :, 3], colt[:, :, 1], relk[:, VOCAB - 1:VOCAB], None, ALU.add))
            own(nc.vector.tensor_tensor(late_sb[:, :, 0:DH], bv_sb[:].rearrange("p (h c) -> p h c", h=NP)[:, :, 0:DH],
                                        relv0[0:1, :].unsqueeze(1).to_broadcast([1, NP, DH]), ALU.add))
            own(nc.vector.tensor_tensor(late_sb[:, :, DH:P], bv_sb[:].rearrange("p (h c) -> p h c", h=NP)[:, :, DH:P],
                                        relv0[0:1, :].unsqueeze(1).to_broadcast([1, NP, DH]), ALU.add))
            dve.wait_ge(alpha_exp, 1)
            own(nc.vector.tensor_scalar(late_sb[:, :, P:LATE], late_sb[:, :, P:LATE], 1.0, None, ALU.add))
            nc.vector.reciprocal(late_sb[:, :, P:LATE], late_sb[:, :, P:LATE]).then_inc(tables, 1)

            STEPS = T * (2 * ROUNDS - 1)

            def divide(it, s):
                wait(dve, normed, T, it, s - 2)
                wait(dve, masked, T, it, s)
                nc.vector.reciprocal(rinv[s % 2][:], rsum[s % 2][:]).then_inc(rinv_done, 1)

            def slot(it, s):
                if there(it, s - 1) and not there(it, s):
                    divide(it, s - 1)
                if not there(it, s):
                    return
                par, r = s % 2, s % BODY
                m = top8[par]

                def own_step(i):
                    dve.wait_ge(top_step, i + 1)

                wait(dve, s_added, 1, it, s)
                settle(dve)
                if there(it, s - 1):
                    dve.wait_ge(top_step, STEPS)
                    dve.sem_clear(top_step)
                step = 0
                for n in range(ROUNDS):
                    for t in range(T):
                        src = s_sb[r][:, t, :] if n == 0 else work[t][:, (n - 1) % 2, :]
                        if n:
                            own_step(step - T)
                        nc.vector.max(m[:, t, 8 * n:8 * n + 8], src).then_inc(top_step, 1)
                        step += 1
                    if n == 0 and there(it, s - 1):
                        divide(it, s - 1)
                    if n < ROUNDS - 1:
                        for t in range(T):
                            src = s_sb[r][:, t, :] if n == 0 else work[t][:, (n - 1) % 2, :]
                            own_step(step - T)
                            nc.vector.match_replace(work[t][:, n % 2, :], m[:, t, 8 * n:8 * n + 8], src,
                                                    LOW).then_inc(top_step, 1)
                            step += 1
                    if n == 0:
                        wait(dve, exp_done, T, it, s - 2)
                        nc.vector.tensor_scalar(nmax[par][:], m[:, :, 0], -1.0, None, ALU.mult).then_inc(nmax_done, 1)
                wait(dve, exp_done, T, it, s)
                wait(dve, t_ready, 1, it, s - BODY)
                wait_dma(dve, diag_out, it, s - BODY)
                wait(dve, left_done, T, it, s - BODY)
                for t in range(T):
                    own_step(step - T + t)
                    nc.vector.scalar_tensor_tensor(a_sb[r][:, t, :], s_sb[r][:, t, :],
                                                   m[:, t, TOPK - 1:TOPK], e_sb[par][:, t, :], ALU.is_ge, ALU.mult,
                                                   accum_out=rsum[par][:, t:t + 1]).then_inc(masked, 1)

            sweep(dve, slot)

            dve.wait_ge(xb_done, 1)
            dve.wait_ge(summed, 4 * HEADS)
            n0 = 2 * TILES + 1
            for i in range(TILES + 4):
                if i < TILES:
                    b, t = divmod(i, T)
                    if i >= T:
                        dve.wait_ge(rT_ready, 2 * (i - T) + 2)
                    nc.vector.tensor_copy(rcur[t][:], res[:, b * H:(b + 1) * H, t, :]).then_inc(rcur_done, 1)
                if 0 <= i - 2 < TILES:
                    j = i - 2
                    dve.wait_ge(y_ready, j + 1)
                    nc.vector.tensor_tensor(y_sb[:, j, :], ps_y[j % T], y_sb[:, j, :], ALU.add).then_inc(y_done, 1)
                if 0 <= i - 3 < TILES:
                    j = i - 3
                    dve.wait_ge(y_done, j + 1)
                    nc.vector.bn_stats(stats[:, j, :], y_sb[:, j, :]).then_inc(row_stats, 1)
                if 0 <= i - 4 < TILES:
                    j = i - 4
                    dve.wait_ge(row_stats, n0 + min(2 * j + 1, 2 * TILES))
                    nc.vector.bn_aggr(mv[:, j, :], stats[:, j, :]).then_inc(row_stats, 1)
            dve.wait_ge(row_stats, n0 + 2 * TILES)
            nc.vector.tensor_scalar(mv[:, :, 1], mv[:, :, 1], EPS, None, ALU.add).then_inc(y_stats, 1)
            dve.wait_ge(std2_done, 1)
            own(nc.vector.reciprocal(rstd[:], std[:]))
            for i in range(TILES):
                nc.vector.tensor_scalar(yn[:, i, :], y_sb[:, i, :], mv[:, i, 0:1], rstd[:, i:i + 1],
                                        ALU.subtract, ALU.mult).then_inc(yn_done, 1)
            for b in range(B):
                dve.wait_ge(f_ready, b + 1)
                nc.vector.tensor_tensor(ffn[:, T * b:T * (b + 1), :],
                                        ps_f[b % 2][:, 0:T * FFN].rearrange("p (t c) -> p t c", t=T),
                                        bffn[:].unsqueeze(1).to_broadcast([P, T, FFN]), ALU.add).then_inc(f_saved, 1)
                if b % (B // 2) == B // 2 - 1:
                    h = b // (B // 2)
                    i = slice(h * TILES // 2, (h + 1) * TILES // 2)
                    dve.wait_ge(f_saved, b + 1)
                    own(nc.vector.tensor_reduce(lmax[:, i], ffn[:, i, DIM:DIM + E_], AX.X, ALU.max))
                    nc.vector.tensor_tensor(gate[:, i, :], ffn[:, i, DIM:DIM + E_],
                                            lmax[:, i].unsqueeze(2).to_broadcast([P, TILES // 2, E_]),
                                            ALU.subtract).then_inc(lmax_done, 1)
            for h in range(2):
                i = slice(h * TILES // 2, (h + 1) * TILES // 2)
                dve.wait_ge(gate_exp, h + 1)
                own(nc.vector.tensor_reduce(gsum[:, i], gate[:, i, :], AX.X, ALU.add))
                own(nc.vector.reciprocal(ginv[:, i], gsum[:, i]))
                own(nc.vector.tensor_tensor(gbf[:, i, :], gate[:, i, :],
                                            ginv[:, i].unsqueeze(2).to_broadcast([P, TILES // 2, E_]), ALU.mult))
                nc.vector.tensor_tensor(z_sb[:, i, :, :], gbf[:, i, :].unsqueeze(3).to_broadcast([P, TILES // 2, E_, R_]),
                                        ffn[:, i, DIM + E_:FFN].unsqueeze(2).to_broadcast([P, TILES // 2, E_, R_]),
                                        ALU.mult).then_inc(z_done, 1)
            for h in range(2):
                dve.wait_ge(by_done, 2 * (h + 1))
                for t in range(T):
                    dve.wait_ge(l_ready, T * h + t + 1)
                    a, e = h * TILES // 2 + t, (h + 1) * TILES // 2
                    nc.vector.tensor_tensor(o_sb[:, a:e:T, :], ps_l[T * h + t].rearrange("p (i d) -> p i d", d=DIM),
                                            y_sb[:, a:e:T, :], ALU.add).then_inc(o_done, 1)

        @block.tensor
        def _(pe):
            mm, transpose = nc.tensor.matmul, nc.tensor.transpose
            pe.wait_ge(made, MADE)
            for g in range(TILES // 4):
                pe.wait_ge(xn_done, 4 * (g + 1))
                if g >= 2:
                    pe.wait_ge(xnT_saved, g - 1)
                for i in range(4):
                    last = transpose(ps_x[g % 2][:, i * P:(i + 1) * P], xn[:, 4 * g + i, :], ident[:])
                last.then_inc(xnT_ready, 1)
            pe.wait_ge(xnT_saved, TILES // 4)
            pe.wait_ge(tables, 1)

            def slot(it, s):
                def power(src, col, saved, ready):
                    par = s % 2
                    for t, c in ((0, 0), (0, 1), (1, 0), (1, 1)):
                        if t == 0:
                            reach_head(saved, s - 2, c)
                        last = mm(ps_r[:, t, col:col + P], aT[par][:, c, t * P:(t + 1) * P],
                                  src[:, c, :, :].rearrange("p h d -> p (h d)"), start=(c == 0), stop=(c == T - 1))
                        if c == T - 1:
                            last.then_inc(ready, 1)

                def reach_head(semaphore, j, c):
                    pe.wait_ge(semaphore, it * (T * BODY) + (T * j + c + 1))

                def scores(t):
                    j = s + 2
                    pair, h = (j // 2) % 2, (j % 2) * DH
                    return mm(ps_s[:, t * N:(t + 1) * N], q_sb[pair][h:h + DH, t * P:(t + 1) * P],
                              k_sb[pair][h:h + DH, t, :], start=True, stop=True)

                if there(it, s + 3):
                    j = s + 3
                    pair, h = (j // 2) % 2, (j % 2) * DH
                    wait_pair(pe, qk_saved, 4, it, j - 2)
                    pe.wait_ge(qk_saved, it * 8 + ((j // 2) * 4 + 1))
                    wait(pe, band_saved, 3, it, j - 1)
                    for t in range(T):
                        last = mm(ps_p[:, t * VOCAB:(t + 1) * VOCAB], q_sb[pair][h:h + DH, t * P:(t + 1) * P],
                                  relk[h:h + DH, :], start=True, stop=True)
                    last.then_inc(p_ready, 1)
                if there(it, s - 2):
                    r = (s - 2) % BODY
                    wait_dma(pe, diag_in, it, s - 2)
                    wait(pe, left_summed, T, it, s - 2)
                    wait(pe, g_saved, 1, it, s - 3)
                    for t in range(T):
                        last = transpose(ps_g[:, t * P:(t + 1) * P], diag[r][:, t, 0:P], ident[:])
                    last.then_inc(g_ready, 1)
                if there(it, s - 2):
                    j = s - 2
                    par, pair = j % 2, (j // 2) % 2
                    wait(pe, t_saved, 1, it, j)
                    wait_pair(pe, v_biased, 1, it, j)
                    wait(pe, r3_saved, 1, it, j - 1)
                    for t in range(T):
                        for c in range(T):
                            mm(ps_r[:, t, 0:P], aT[par][:, c, t * P:(t + 1) * P], v_sb[pair][:, c, :],
                               start=(c == 0), stop=False)
                if there(it, s - 2):
                    par = s % 2
                    wait(pe, g_saved, 1, it, s - 2)
                    for t in range(T):
                        mm(ps_r[:, t, 0:P], diagT[par][:, t * P:(t + 1) * P], relv[:].rearrange("p h d -> p (h d)"),
                           start=False, stop=True).then_inc(r1_ready, 1)
                if there(it, s + 2):
                    wait_pair(pe, qk_saved, 4, it, s + 2)
                    wait(pe, s_saved, 1, it, s + 1)
                    scores(0)
                if there(it, s - 2):
                    power(v1, P, r1_saved, r2_ready)
                if there(it, s - 1):
                    r, par = (s - 1) % BODY, (s - 1) % 2
                    wait(pe, normed, T, it, s - 1)
                    wait(pe, t_saved, 1, it, s - 2)
                    for c in range(T):
                        for t in range(T):
                            last = transpose(ps_t[:, c * N + t * P:c * N + (t + 1) * P],
                                             a_sb[r][:, t, c * P:(c + 1) * P], ident[:])
                    last.then_inc(t_ready, 1)
                if s % 2 == 0 and there(it, s + 4):
                    pair = (s // 2) % 2
                    wait_pair_dma(pe, pair_in, 48, it, s + 4)
                    wait_pair(pe, qk_saved, 4, it, s + 2)
                    mm(ps_qk[:, 0:N], w_sb[pair][:, 0:P], xT[pair][:], start=True, stop=True)
                    mm(ps_qk[:, N:2 * N], w_sb[pair][:, P:2 * P], xT[pair][:], start=True,
                       stop=True).then_inc(qk_ready, 1)
                if there(it, s - 2):
                    power(v2, 2 * P, r2_saved, r3_ready)
                if there(it, s + 2):
                    scores(1).then_inc(s_ready, 1)
                if s % 2 == 0 and there(it, s + 2):
                    pair = ((s + 2) // 2) % 2
                    wait_pair(pe, v_saved, 1, it, s)
                    for c in range(T):
                        last = mm(ps_v[:, c * P:(c + 1) * P], xT[pair][:, c * P:(c + 1) * P],
                                  w_sb[pair][:, 2 * P:3 * P], start=True, stop=True)
                    last.then_inc(v_ready, 1)

            sweep(pe, slot)

            pe.wait_ge(r3_saved, HEADS)
            pe.wait_ge(s_saved, HEADS)
            pe.wait_ge(qk_saved, 4 * HEADS // 2)
            def gathered(b, t):
                i = b * T + t
                pe.wait_ge(rcur_done, i + 1)
                for half in range(2):
                    reach(pe, rT_saved, 2 * i + half - 1)
                    for k in range(NP // 2):
                        h = half * NP // 2 + k
                        last = transpose(ps_x[half][:, k * P:(k + 1) * P],
                                         rcur[t][:, 2 * h:2 * h + 2, :].rearrange("p a d -> p (a d)"), ident[:])
                    last.then_inc(rT_ready, 1)

            def project(b, t):
                i = b * T + t
                pe.wait_ge(rT_saved, 2 * i + 2)
                reach(pe, y_done, i - T + 1)
                for h in range(NP):
                    last = mm(ps_y[t], rT[t][:, h, :], wout[:, h, :], start=(h == 0), stop=(h == NP - 1))
                last.then_inc(y_ready, 1)

            def layer(b):
                pe.wait_ge(ynT_saved, b // 2 + 1)
                if b >= 2:
                    pe.wait_ge(f_saved, b - 1)
                for t in range(T):
                    i = b * T + t
                    last = mm(ps_f[b % 2][:, t * FFN:(t + 1) * FFN], ynT[:, i * P:(i + 1) * P], wffn[:],
                              start=True, stop=True)
                last.then_inc(f_ready, 1)

            gathered(0, 0)
            gathered(0, 1)
            project(0, 0)

            def batch(b):
                gathered(b, 0)
                project(b - 1, 1)
                gathered(b, 1)
                project(b, 0)

            batch(1)
            with pe.Fori(2, B) as b:
                batch(b)
            project(B - 1, 1)

            for g in range(TILES // 4):
                pe.wait_ge(yn_done, 4 * (g + 1))
                if g >= 2:
                    pe.wait_ge(ynT_saved, g - 1)
                for i in range(4):
                    last = transpose(ps_x[g % 2][:, i * P:(i + 1) * P], yn[:, 4 * g + i, :], ident[:])
                last.then_inc(ynT_ready, 1)
                if g:
                    layer(2 * g - 2)
                    layer(2 * g - 1)
            layer(B - 2)
            layer(B - 1)
            for h in range(2):
                pe.wait_ge(z_done, h + 1)
                for k in range(B // 2):
                    b = h * B // 2 + k
                    last = transpose(ps_x[h][:, k * P:(k + 1) * P],
                                     z_sb[:, T * b:T * (b + 1), :, :].rearrange("p t e r -> p (t e r)"), ident[:])
                last.then_inc(zT_ready, 1)
            for h in range(2):
                pe.wait_ge(zT_saved, h + 1)
                for t in range(T):
                    z = slice(t * E_ * R_, (t + 1) * E_ * R_)
                    for k in range(B // 2):
                        last = mm(ps_l[T * h + t][:, k * DIM:(k + 1) * DIM], zT[z, h * B // 2 + k, :], lorab[z, :],
                                  start=True, stop=True)
                    last.then_inc(l_ready, 1)


def kernel(L0_attn_x, L0_attn_Wqkv, L0_attn_bqkv, L0_attn_Wout, L0_attn_bout, L0_attn_rel_k_emb,
           L0_attn_rel_v_emb, L0_attn_alphas_raw, L0_ffn_base_w, L0_ffn_base_b, L0_ffn_lora_A, L0_ffn_lora_B,
           L0_ffn_router_w, L0_ffn_router_b):
    import concourse.bacc as bacc
    from concourse.bass_utils import run_bass_kernel_spmd

    f = {k: np.asarray(v) for k, v in dict(
        x=L0_attn_x, wqkv=L0_attn_Wqkv, bqkv=L0_attn_bqkv, wout=L0_attn_Wout, bout=L0_attn_bout,
        relk=L0_attn_rel_k_emb, relv=L0_attn_rel_v_emb, alphas=L0_attn_alphas_raw, bw=L0_ffn_base_w,
        bb=L0_ffn_base_b, la=L0_ffn_lora_A, lb=L0_ffn_lora_B, rw=L0_ffn_router_w, rb=L0_ffn_router_b).items()}
    inner, dim = f["wqkv"].shape[0] // 3, f["wqkv"].shape[1]
    pairs = inner // 128
    w = f["wqkv"].reshape(3, pairs, 128, dim).transpose(1, 3, 0, 2).reshape(pairs, dim, 3 * 128)
    bqk = f["bqkv"].reshape(3, pairs, 128)[:2].transpose(1, 2, 0)
    ins = {
        "x": f["x"],
        "wqkv": np.concatenate([w, bqk], axis=2),
        "bv": f["bqkv"][None, 2 * inner:],
        "wout": f["wout"].T,
        "bout": f["bout"][None, :],
        "relk": f["relk"][::-1].T,
        "relv": f["relv"][::-1],
        "alphas": f["alphas"].T.reshape(1, -1),
        "wffn": np.concatenate([f["bw"].T, f["rw"].T, f["la"]], axis=1),
        "bffn": np.concatenate([f["bb"], f["rb"]])[None, :],
        "lorab": f["lb"].reshape(-1, f["lb"].shape[2]),
    }
    nc = bacc.Bacc("TRN2", target_bir_lowering=False, num_devices=1)
    arrays, args = {}, []
    for name, a in ins.items():
        a = np.ascontiguousarray(a)
        arrays[f"in_{name}"] = a
        args.append(nc.dram_tensor(f"in_{name}", a.shape, mybir.dt.from_np(a.dtype), kind="ExternalInput").ap())
    args.append(nc.dram_tensor("out_0", f["x"].shape, mybir.dt.float32, kind="ExternalOutput").ap())
    preln_attention_ffn(nc, *args)
    r = run_bass_kernel_spmd(nc, [arrays], core_ids=[0])
    return r.results[0]["out_0"]
```
